# Optimizing a Trainium2 kernel written in Bass

```python
import numpy as np
import jax
import jax.numpy as jnp

def _softmax(x, axis=-1):
    return jax.nn.softmax(x, axis=axis)

def _gelu(x):
    return jax.nn.gelu(x, approximate=True)

def _silu(x):
    return jax.nn.silu(x)

def _sigmoid(x):
    return jax.nn.sigmoid(x)

def _layernorm(x, axis=-1, eps=1e-05):
    m = jnp.mean(x, axis=axis, keepdims=True)
    v = jnp.var(x, axis=axis, keepdims=True)
    return (x - m) / jnp.sqrt(v + eps)

def _scatter_add(tgt, idx, src, axis=0):
    return tgt.at[idx].add(src)

def _segment_sum(src, seg, n):
    return jax.ops.segment_sum(src, seg, n)
kernel_name = 'mk_prb_d1_jaxref_r8_8e4cc3'

def setup_inputs(seed: int=0):
    np.random.seed(seed)
    _w = jnp.asarray

    def _L0_attn_setup():
        import jax, jax.numpy as jnp
        import numpy as np
        import math
        D_MODEL = 128
        D_QUERY = 64
        key = jax.random.key(seed)
        k1, k2, k3, k4 = jax.random.split(key, 4)
        X = jax.random.normal(k1, (4, 512, D_MODEL), dtype=jnp.float32)
        Wq = jax.random.normal(k2, (D_MODEL, D_QUERY), dtype=jnp.float32) * (1.0 / math.sqrt(D_MODEL))
        Wk = jax.random.normal(k3, (D_MODEL, D_QUERY), dtype=jnp.float32) * (1.0 / math.sqrt(D_MODEL))
        Wv = jax.random.normal(k4, (D_MODEL, D_MODEL), dtype=jnp.float32) * (1.0 / math.sqrt(D_MODEL))
        return {'X': X, 'Wq': Wq, 'Wk': Wk, 'Wv': Wv}
    _L0_attn_in = _L0_attn_setup()

    def _L0_ffn_setup():
        import jax, jax.numpy as jnp
        import numpy as np
        DIM = 128
        DEPTH = 6
        HEADS = 16
        DIM_HEAD = 64
        WINDOW = 32
        INNER = HEADS * DIM_HEAD
        DIM_INNER = int(DIM * 4 * 2 / 3)
        QK_SCALE = 8.0

        def shift_tokens(t):
            a, s = jnp.split(t, 2, -1)
            s = jnp.pad(s, ((0, 0), (1, 0), (0, 0)))[:, :-1]
            return jnp.concatenate([a, s], -1)

        def l2norm(t):
            return t / jnp.maximum(jnp.linalg.norm(t, axis=-1, keepdims=True), 1e-12)

        def rotate_half(x):
            x1, x2 = jnp.split(x, 2, -1)
            return jnp.concatenate([-x2, x1], -1)

        def rotary_tables(n):
            half = jnp.arange(0, DIM_HEAD, 2, dtype=jnp.float32)
            inv_freq = 1.0 / 10000.0 ** (half / DIM_HEAD)
            t = jnp.arange(n, dtype=jnp.float32)
            freqs = t[:, None] * inv_freq[None, :]
            freqs = jnp.concatenate([freqs, freqs], -1)
            base_scale = (half + 0.4 * DIM_HEAD) / (1.4 * DIM_HEAD)
            power = (t - n // 2) / (WINDOW // 2)
            scale = base_scale[None, :] ** power[:, None]
            scale = jnp.concatenate([scale, scale], -1)
            return (freqs, scale)

        def local_attention(q, k, v):
            b, h, n, d = q.shape
            w = WINDOW
            nw = n // w
            bq = q.reshape(b, h, nw, w, d)
            bk = k.reshape(b, h, nw, w, d)
            bv = v.reshape(b, h, nw, w, d)

            def look(t):
                p = jnp.pad(t, ((0, 0), (0, 0), (1, 0), (0, 0), (0, 0)))
                return jnp.concatenate([p[:, :, :nw], p[:, :, 1:]], axis=3)
            bk2, bv2 = (look(bk), look(bv))
            seq = jnp.arange(n).reshape(nw, w)
            seq_p = jnp.pad(seq, ((1, 0), (0, 0)), constant_values=-1)
            jt = jnp.concatenate([seq_p[:nw], seq_p[1:]], axis=1)
            it = seq[:, :, None]
            jb = jt[:, None, :]
            mask = (it < jb) | (it > jb + w) | (jb == -1)
            sim = jnp.einsum('bhwie,bhwje->bhwij', bq, bk2) * QK_SCALE
            sim = jnp.where(mask, -jnp.finfo(sim.dtype).max, sim)
            attn = jax.nn.softmax(sim, -1)
            out = jnp.einsum('bhwij,bhwje->bhwie', attn, bv2)
            return out.reshape(b, h, n, d)

        def attn_layer(x, Wqkv, qs, ksc, Wo):
            b, n, _ = x.shape
            qkv = x @ Wqkv
            q, k, v = jnp.split(qkv, 3, -1)
            sh = lambda t: t.reshape(b, n, HEADS, DIM_HEAD).transpose(0, 2, 1, 3)
            q, k, v = (sh(q), sh(k), sh(v))
            q = l2norm(q) * qs
            k = l2norm(k) * ksc
            freqs, scale = rotary_tables(n)
            cos, sin = (jnp.cos(freqs), jnp.sin(freqs))
            q = q * cos * scale + rotate_half(q) * sin * scale
            inv = 1.0 / scale
            k = k * cos * inv + rotate_half(k) * sin * inv
            out = local_attention(q, k, v)
            out = out.transpose(0, 2, 1, 3).reshape(b, n, INNER)
            return out @ Wo

        def ffn_layer(x, g, bln, W1, b1, W2, b2):
            mu = x.mean(-1, keepdims=True)
            var = ((x - mu) ** 2).mean(-1, keepdims=True)
            xn = (x - mu) / jnp.sqrt(var + 1e-05) * g + bln
            hg = xn @ W1 + b1
            a, gate = jnp.split(hg, 2, -1)
            return a * jax.nn.gelu(gate, approximate=False) @ W2 + b2
        key = jax.random.key(seed)
        ks = jax.random.split(key, 8)
        B, N = (2, 256)
        init = lambda k, shape: jax.random.normal(k, shape, jnp.float32) * 0.02
        return {'x': jax.random.normal(ks[0], (B, N, DIM), jnp.float32), 'Wqkv': init(ks[1], (DEPTH, DIM, 3 * INNER)), 'q_scale': jnp.ones((DEPTH, DIM_HEAD), jnp.float32), 'k_scale': jnp.ones((DEPTH, DIM_HEAD), jnp.float32), 'Wo': init(ks[2], (DEPTH, INNER, DIM)), 'ln_g': jnp.ones((DEPTH, DIM), jnp.float32), 'ln_b': jnp.zeros((DEPTH, DIM), jnp.float32), 'W1': init(ks[3], (DEPTH, DIM, 2 * DIM_INNER)), 'b1': jnp.zeros((DEPTH, 2 * DIM_INNER), jnp.float32), 'W2': init(ks[4], (DEPTH, DIM_INNER, DIM)), 'b2': jnp.zeros((DEPTH, DIM), jnp.float32)}
    _L0_ffn_in = _L0_ffn_setup()
    _d = {'L0_attn_X': _L0_attn_in['X'], 'L0_attn_Wq': _L0_attn_in['Wq'], 'L0_attn_Wk': _L0_attn_in['Wk'], 'L0_attn_Wv': _L0_attn_in['Wv'], 'L0_ffn_Wqkv': _L0_ffn_in['Wqkv'], 'L0_ffn_q_scale': _L0_ffn_in['q_scale'], 'L0_ffn_k_scale': _L0_ffn_in['k_scale'], 'L0_ffn_Wo': _L0_ffn_in['Wo'], 'L0_ffn_ln_g': _L0_ffn_in['ln_g'], 'L0_ffn_ln_b': _L0_ffn_in['ln_b'], 'L0_ffn_W1': _L0_ffn_in['W1'], 'L0_ffn_b1': _L0_ffn_in['b1'], 'L0_ffn_W2': _L0_ffn_in['W2'], 'L0_ffn_b2': _L0_ffn_in['b2']}
    _x0 = _d['L0_attn_X']
    _d['L0_attn_X'] = jax.random.normal(jax.random.fold_in(jax.random.key(seed), 1), (8, 512, 128), dtype=_x0.dtype)
    del _x0
    return _d

def reference(L0_attn_X, L0_attn_Wq, L0_attn_Wk, L0_attn_Wv, L0_ffn_Wqkv, L0_ffn_q_scale, L0_ffn_k_scale, L0_ffn_Wo, L0_ffn_ln_g, L0_ffn_ln_b, L0_ffn_W1, L0_ffn_b1, L0_ffn_W2, L0_ffn_b2):

    def _L0_attn_ref(X, Wq, Wk, Wv):
        import jax, jax.numpy as jnp
        import numpy as np
        import math
        D_MODEL = 128
        D_QUERY = 64
        B, T, _ = X.shape
        Q = X @ Wq
        K = X @ Wk
        V = X @ Wv
        scores = jnp.einsum('btd,bsd->bts', Q, K)
        causal = jnp.tril(jnp.ones((T, T), dtype=bool))
        scores = jnp.where(causal[None, :, :], scores, -jnp.inf)
        attn = jax.nn.softmax(scores / math.sqrt(D_QUERY), axis=2)
        return attn @ V

    def _L0_ffn_ref(x, Wqkv, q_scale, k_scale, Wo, ln_g, ln_b, W1, b1, W2, b2):
        import jax, jax.numpy as jnp
        import numpy as np
        DIM = 128
        DEPTH = 6
        HEADS = 16
        DIM_HEAD = 64
        WINDOW = 32
        INNER = HEADS * DIM_HEAD
        DIM_INNER = int(DIM * 4 * 2 / 3)
        QK_SCALE = 8.0

        def shift_tokens(t):
            a, s = jnp.split(t, 2, -1)
            s = jnp.pad(s, ((0, 0), (1, 0), (0, 0)))[:, :-1]
            return jnp.concatenate([a, s], -1)

        def l2norm(t):
            return t / jnp.maximum(jnp.linalg.norm(t, axis=-1, keepdims=True), 1e-12)

        def rotate_half(x):
            x1, x2 = jnp.split(x, 2, -1)
            return jnp.concatenate([-x2, x1], -1)

        def rotary_tables(n):
            half = jnp.arange(0, DIM_HEAD, 2, dtype=jnp.float32)
            inv_freq = 1.0 / 10000.0 ** (half / DIM_HEAD)
            t = jnp.arange(n, dtype=jnp.float32)
            freqs = t[:, None] * inv_freq[None, :]
            freqs = jnp.concatenate([freqs, freqs], -1)
            base_scale = (half + 0.4 * DIM_HEAD) / (1.4 * DIM_HEAD)
            power = (t - n // 2) / (WINDOW // 2)
            scale = base_scale[None, :] ** power[:, None]
            scale = jnp.concatenate([scale, scale], -1)
            return (freqs, scale)

        def local_attention(q, k, v):
            b, h, n, d = q.shape
            w = WINDOW
            nw = n // w
            bq = q.reshape(b, h, nw, w, d)
            bk = k.reshape(b, h, nw, w, d)
            bv = v.reshape(b, h, nw, w, d)

            def look(t):
                p = jnp.pad(t, ((0, 0), (0, 0), (1, 0), (0, 0), (0, 0)))
                return jnp.concatenate([p[:, :, :nw], p[:, :, 1:]], axis=3)
            bk2, bv2 = (look(bk), look(bv))
            seq = jnp.arange(n).reshape(nw, w)
            seq_p = jnp.pad(seq, ((1, 0), (0, 0)), constant_values=-1)
            jt = jnp.concatenate([seq_p[:nw], seq_p[1:]], axis=1)
            it = seq[:, :, None]
            jb = jt[:, None, :]
            mask = (it < jb) | (it > jb + w) | (jb == -1)
            sim = jnp.einsum('bhwie,bhwje->bhwij', bq, bk2) * QK_SCALE
            sim = jnp.where(mask, -jnp.finfo(sim.dtype).max, sim)
            attn = jax.nn.softmax(sim, -1)
            out = jnp.einsum('bhwij,bhwje->bhwie', attn, bv2)
            return out.reshape(b, h, n, d)

        def attn_layer(x, Wqkv, qs, ksc, Wo):
            b, n, _ = x.shape
            qkv = x @ Wqkv
            q, k, v = jnp.split(qkv, 3, -1)
            sh = lambda t: t.reshape(b, n, HEADS, DIM_HEAD).transpose(0, 2, 1, 3)
            q, k, v = (sh(q), sh(k), sh(v))
            q = l2norm(q) * qs
            k = l2norm(k) * ksc
            freqs, scale = rotary_tables(n)
            cos, sin = (jnp.cos(freqs), jnp.sin(freqs))
            q = q * cos * scale + rotate_half(q) * sin * scale
            inv = 1.0 / scale
            k = k * cos * inv + rotate_half(k) * sin * inv
            out = local_attention(q, k, v)
            out = out.transpose(0, 2, 1, 3).reshape(b, n, INNER)
            return out @ Wo

        def ffn_layer(x, g, bln, W1, b1, W2, b2):
            mu = x.mean(-1, keepdims=True)
            var = ((x - mu) ** 2).mean(-1, keepdims=True)
            xn = (x - mu) / jnp.sqrt(var + 1e-05) * g + bln
            hg = xn @ W1 + b1
            a, gate = jnp.split(hg, 2, -1)
            return a * jax.nn.gelu(gate, approximate=False) @ W2 + b2
        for i in range(DEPTH):
            x = attn_layer(shift_tokens(x), Wqkv[i], q_scale[i], k_scale[i], Wo[i]) + x
            x = ffn_layer(shift_tokens(x), ln_g[i], ln_b[i], W1[i], b1[i], W2[i], b2[i]) + x
        return x
    x = L0_attn_X
    xn = _layernorm(x, axis=-1)
    x = x + _L0_attn_ref(xn, L0_attn_Wq, L0_attn_Wk, L0_attn_Wv) + _L0_ffn_ref(xn, L0_ffn_Wqkv, L0_ffn_q_scale, L0_ffn_k_scale, L0_ffn_Wo, L0_ffn_ln_g, L0_ffn_ln_b, L0_ffn_W1, L0_ffn_b1, L0_ffn_W2, L0_ffn_b2)
    return x

_drawn_inputs = setup_inputs


def setup_inputs(seed=0):
    import zlib

    import numpy as np

    out = dict(_drawn_inputs(seed))
    spreads = {'L0_ffn_q_scale': (1.0, 0.6),
     'L0_ffn_k_scale': (1.0, 0.6),
     'L0_ffn_ln_g': (1.0, 0.6),
     'L0_ffn_ln_b': (0.0, 0.8),
     'L0_ffn_b1': (0.0, 0.8),
     'L0_ffn_b2': (0.0, 0.1)}
    factors = {'L0_ffn_W1': 3.654, 'L0_ffn_W2': 3.589}
    for name, (base, spread) in spreads.items():
        noise = np.random.default_rng([zlib.crc32(name.encode()), seed]).standard_normal(out[name].shape)
        drawn = base * np.exp(spread * noise) if base else spread * noise
        out[name] = jnp.asarray(drawn.astype(out[name].dtype))
    for name, factor in factors.items():
        out[name] = (out[name] * factor).astype(out[name].dtype)
    return out
```

```python
import math
from contextlib import ExitStack

import concourse.bass as bass
import numpy as np
from concourse import mybir

F32, F32R, BF16, I32 = mybir.dt.float32, mybir.dt.float32r, mybir.dt.bfloat16, mybir.dt.int32
ACT, ALU, AX = mybir.ActivationFunctionType, mybir.AluOpType, mybir.AxisListType

BATCH, SEQ, DIM = 8, 512, 128
DEPTH, HEADS, DH, WIN = 6, 16, 64, 32
INNER = HEADS * DH
FF = 341
FC = 114
NFC = 3
FROWS = [FC, FC, FF - 2 * FC]
TILES = SEQ // 128
UPB = 2 * TILES
BODIES = DEPTH * BATCH
NUNITS, NTILES = BODIES * UPB, BODIES * TILES
SW = SEQ + 2
DQ = 64
SQRT_MAGIC = float(0x5F3759DF)
NEWTON = 11
MASKED = -1e30
T_LAG, P_LAG, O_LAG, WO_LAG = 3, 4, 5, 7


def build(nc, X, Wq, Wk, Wv, Wqkv, q_scale, k_scale, Wo, ln_g, ln_b, W1, b1, W2, b2,
          rot_tables, window_mask, causal_mask, eye, eye_bf, out):
    ctx = ExitStack()
    with ctx:
        def sb(name, shape, dt=F32):
            return ctx.enter_context(nc.sbuf_tensor(name, shape, dt))

        def sem(name):
            return ctx.enter_context(nc.semaphore(name))

        xs = sb("xs", [128, BATCH * SW])
        wqkv_raw = sb("wqkv_raw", [128, 3 * INNER])
        wqkv_hi = sb("wqkv_hi", [128, 3 * INNER], F32R)
        wqkv_lo = sb("wqkv_lo", [128, 3 * INNER], F32R)
        wo_sb = sb("wo_sb", [128, HEADS // 2, DIM])
        w1_raw = sb("w1_raw", [128, 2 * FF])
        w1_hi = sb("w1_hi", [128, 2 * FF], F32R)
        w1_lo = sb("w1_lo", [128, 2 * FF], F32R)
        w2_sb = sb("w2_sb", [FC, NFC, DIM])
        b1_sb = sb("b1_sb", [FC, 2, NFC])
        b2_sb = sb("b2_sb", [128, 1])
        lng_sb = sb("lng_sb", [128, 1])
        lnb_sb = sb("lnb_sb", [128, 1])
        rot_base = sb("rot_base", [128, 4, TILES, DH])
        rot = sb("rot", [128, 4, TILES, DH])
        qks = sb("qks", [128, 4, DEPTH, DH])
        mask_w = sb("mask_w", [128, 2, 256], BF16)
        mask_c = sb("mask_c", [128, SEQ], BF16)
        ident = sb("ident", [128, 128])
        ident_b = sb("ident_b", [128, 128], BF16)
        xh = sb("xh", [128, SEQ], F32R)
        xl = sb("xl", [128, SEQ], F32R)
        sq = sb("sq", [128, 2, 512])
        t1 = sb("t1", [128, 2, 2, 512])
        t2 = sb("t2", [128, 2, 2, 512])
        qk = sb("qk", [128, 4, 2, 512])
        n2 = sb("n2", [128, 2, 16])
        nwt = sb("nwt", [128, 16])
        rn = sb("rn", [128, 4, 16])
        qT = sb("qT", [128, 2, 4, 128])
        kT = sb("kT", [128, 2, 2, 4, WIN + 128])
        smax = sb("smax", [128, 2, 8])
        dsub = sb("dsub", [128, 2, 512])
        prob = sb("prob", [128, 2, 512])
        rsum = sb("rsum", [128, 2, 8])
        rinv = sb("rinv", [128, 2, 8])
        pT = sb("pT", [128, 2, 4, 128])
        v_sb = sb("v_sb", [128, 2, 2, 512])
        vw = sb("vw", [128, 2, 4, 512])
        o_sb = sb("o_sb", [128, 2, 512])
        oT = sb("oT", [128, 2, 8, 128])
        x2 = sb("x2", [128, SEQ])
        xt = sb("xt", [128, TILES, 128])
        bst = sb("bst", [128, TILES, 6])
        mv = sb("mv", [128, TILES, 2])
        lnt = sb("lnt", [128, TILES])
        lnr = sb("lnr", [128, TILES])
        lnv = sb("lnv", [128, TILES])
        xn = sb("xn", [128, SEQ])
        xn_hi = sb("xn_hi", [128, SEQ], F32R)
        xn_lo = sb("xn_lo", [128, SEQ], F32R)
        gate = sb("gate", [FC, NFC, SEQ])
        hid = sb("hid", [FC, NFC, SEQ])
        xin = t1[:, :, :, :].rearrange("p a b (c d) -> p (a b) c d", c=TILES)
        wq_sb = wqkv_raw[:, 0:2 * DQ].rearrange("p (a d) -> p a d", a=2)
        wv_sb = wqkv_raw[:, 2 * DQ:2 * DQ + DIM]
        last_q = qk[0:DQ, 0, 0, :]
        last_k = qk[0:DQ, 0, 1, :]
        last_v = qk[:, 1, 0, :].rearrange("p (t d) -> p t d", t=TILES)
        last_p = qk[:, 2, :, :]
        last_pT = qk[:, 3, :, :]
        last_f = dsub
        last_acc = prob
        last_o = o_sb

        ps = ctx.enter_context(nc.psum_tensor("ps", [128, 8, 512], F32))
        P_BANK, T_BANK, S_BANK, W0, W1B = (0, 1), (2, 3), 4, ps[:, 6, :], ps[:, 7, :]

        projected, squared, rotated, reduced = sem("projected"), sem("squared"), sem("rotated"), sem("reduced")
        v_copied, summed, newton, normed = sem("v_copied"), sem("summed"), sem("newton"), sem("normed")
        xh_ready, xl_ready = sem("xh_ready"), sem("xl_ready")
        tq, tk, tp, to, tlf, tlb = (sem(f"transposed_{x}") for x in ("q", "k", "p", "o", "ln", "lnb"))
        cq, ck, cp, co, clf, clb = (sem(f"copied_{x}") for x in ("q", "k", "p", "o", "ln", "lnb"))
        scored, maxed, subbed, expd = sem("scored"), sem("maxed"), sem("subbed"), sem("expd")
        sumd, inverted, attended, o_copied = sem("sumd"), sem("inverted"), sem("attended"), sem("o_copied")
        clamped = sem("clamped")
        vw_edge, vw_ready = [sem(f"vw_edge{s}") for s in range(2)], [sem(f"vw_ready{s}") for s in range(2)]
        wo_done, res1 = sem("wo_done"), sem("res1")
        x2_ready, bn_done, ag_done, ln_newton, xt_normed = sem("x2_ready"), sem("bn_done"), sem("ag_done"), sem("ln_newton"), sem("xt_normed")
        xnh_ready, xnl_ready = sem("xnh_ready"), sem("xnl_ready")
        gate_done, gate_copied, a_done, a_copied = sem("gate_done"), sem("gate_copied"), sem("a_done"), sem("a_copied")
        gelu_done, hid_done, down_done, res2 = sem("gelu_done"), sem("hid_done"), sem("down_done"), sem("res2")
        raw_in, wsplit_hi, wsplit_lo, rot_ready = sem("raw_in"), sem("wsplit_hi"), sem("wsplit_lo"), sem("rot_ready")
        w1raw_in, w1_hi_ready, w1_lo_ready = sem("w1raw_in"), sem("w1_hi_ready"), sem("w1_lo_ready")
        wo_in, lnp_in, ffp_in, const_in, zeroed = sem("wo_in"), sem("lnp_in"), sem("ffp_in"), sem("const_in"), sem("zeroed")
        x_in = [sem(f"first_x{j}") for j in range(2)]
        f_bn, f_ag, f_newton, f_norm, f_tr, f_cp = (sem(f"first_{x}") for x in ("bn", "ag", "newton", "norm", "tr", "cp"))
        l_x, l_out = [sem(f"last_x{j}") for j in range(2)], [sem(f"last_out{j}") for j in range(2)]
        l_bn, l_ag, l_newton, l_norm, l_tr, l_cp = (sem(f"last_{x}") for x in ("bn", "ag", "newton", "norm", "tr", "cp"))
        l_w = sem("last_w")
        l_mm, l_ev, l_fs, l_ft, l_s, l_mx, l_ng, l_ex, l_iv, l_pt, l_pc, l_o, l_acc, l_res = (
            sem(f"last_{x}") for x in ("mm", "ev", "fs", "ft", "s", "mx", "ng", "ex", "iv", "pt", "pc", "o", "acc", "res"))

        CONSTS = 11

        def wait(e, s, value):
            if not isinstance(value, int) or value > 0:
                e.wait_ge(s, value)

        def at_most(value, total):
            return min(value, total) if isinstance(value, int) else value

        def live(i, total):
            return not isinstance(i, int) or 0 <= i < total

        def bodies(e, body):
            for b in range(3):
                body(b, b, 0)
            with e.Fori(3, BATCH) as b:
                body(b, b, 0)
            with e.Fori(1, DEPTH) as layer:
                body(layer * BATCH, 0, layer)
                body(layer * BATCH + 1, 1, layer)
                with e.Fori(2, BATCH) as b:
                    body(layer * BATCH + b, b, layer)
            body(BODIES, 0, None)
            body(BODIES + 1, 1, None)

        def pairs(e, body):
            for j in range(2):
                body(j, j, 0)
            with e.Fori(1, BATCH // 2) as pair:
                for j in range(2):
                    body(pair * 2 + j, j, pair)

        def unit(g, n, lag):
            return g * UPB + (n - lag)

        def slot(n, lag, size):
            return (n - lag) % size

        def half(n, lag):
            return (n - lag) % 2

        def tslot(n, lag):
            return (n - lag) % UPB // 2

        T_USES = []
        for n in range(UPB):
            T_USES += [("q", n), ("k", n)]
            if n == 1:
                T_USES.append(("lnb", 1))
            T_USES += [("o", n), ("p", n)]
            if n == 6:
                T_USES.append(("ln", 6))
        T_LAGS = {"q": T_LAG, "k": T_LAG, "p": P_LAG, "o": O_LAG}
        T_COPIED = {"q": cq, "k": ck, "p": cp, "o": co, "ln": clf, "lnb": clb}

        def t_bank(kind, n):
            return T_BANK[T_USES.index((kind, n)) % 2]

        def t_free(e, g, kind, n):
            i = T_USES.index((kind, n)) - 2
            k2, n2_ = T_USES[i % len(T_USES)]
            g2 = g if i >= 0 else g - 1
            if k2 == "ln":
                wait(e, clf, at_most(g2, BODIES))
            elif k2 == "lnb":
                wait(e, clb, g2 - 1)
            else:
                wait(e, T_COPIED[k2], at_most(unit(g2, n2_, T_LAGS[k2]) + 1, NUNITS))

        def prev_batch(b, k):
            return (b - k) % BATCH if isinstance(b, int) else b - k

        def state(b, lo, width, part=slice(0, 128)):
            return xs[part, bass.ds(b * SW + lo, width)]

        def raw_chunk(kind, h):
            w = wqkv_raw[:, kind * INNER:(kind + 1) * INNER]
            if kind < 2:
                return w[:, h * 512:h * 512 + 512]
            return w.rearrange("p (a b d) -> p b a d", b=2, d=DH)[:, h]

        def chunk(w, kind, h):
            return w[:, (2 * kind + h) * 512:(2 * kind + h) * 512 + 512]

        def view_v(c):
            return c.rearrange("p (a d) -> p a d", d=DH)

        block = ctx.enter_context(nc.Block())

        @block.sync
        def _(sp):
            def load_raw(layer):
                if not isinstance(layer, int):
                    sp.wait_ge(wsplit_lo, layer * 6)
                    sp.wait_ge(w1_lo_ready, layer)
                sp.dma_start(wqkv_raw[:, :], Wqkv[bass.ds(layer, 1), :, :].rearrange("l p n -> p (l n)")).then_inc(raw_in, 16)
                sp.dma_start(w1_raw[:, :], W1[bass.ds(layer, 1), :, :].rearrange("l p n -> p (l n)")).then_inc(w1raw_in, 16)

            def load_wo(layer):
                if not isinstance(layer, int):
                    sp.wait_ge(wo_done, layer * (BATCH * TILES))
                sp.dma_start(wo_sb[:, :, :], Wo[bass.ds(layer, 1), :, :].rearrange("l (c p) n -> p (l c) n", p=128)).then_inc(wo_in, 16)

            def load_ln(layer):
                if not isinstance(layer, int):
                    sp.wait_ge(clb, layer * BATCH)
                sp.dma_start(lng_sb[:, :], ln_g[bass.ds(layer, 1), :].rearrange("l p -> p l")).then_inc(lnp_in, 16)
                sp.dma_start(lnb_sb[:, :], ln_b[bass.ds(layer, 1), :].rearrange("l p -> p l")).then_inc(lnp_in, 16)

            def load_ff(layer):
                if not isinstance(layer, int):
                    sp.wait_ge(res2, layer * BATCH)
                for c, rows in enumerate(FROWS):
                    sp.dma_start(w2_sb[0:rows, c, :], W2[bass.ds(layer, 1), c * FC:c * FC + rows, :].rearrange("l p n -> p (l n)")).then_inc(ffp_in, 16)
                    for a in range(2):
                        src = b1[bass.ds(layer, 1), a * FF + c * FC:a * FF + c * FC + rows]
                        sp.dma_start(b1_sb[0:rows, a, c:c + 1], src.rearrange("l p -> p l")).then_inc(ffp_in, 16)
                sp.dma_start(b2_sb[:, :], b2[bass.ds(layer, 1), :].rearrange("l p -> p l")).then_inc(ffp_in, 16)

            def windows(tile, s):
                copied, used = tile * 2 + 2, tile * 2 - 2
                if not isinstance(tile, int):
                    copied, used = sp.to_reg(copied), sp.to_reg(used)
                sp.wait_ge(v_copied, copied)
                wait(sp, attended, used)
                for par in range(2):
                    sp.dma_start(vw[par * 64:par * 64 + WIN, s, 0, :], v_sb[96:128, 1 - s, par, :]).then_inc(vw_edge[s], 16)
                for par in range(2):
                    to_row = par * 64
                    sp.dma_start(vw[to_row + WIN:to_row + 64, s, 0, :], v_sb[0:WIN, s, par, :]).then_inc(vw_ready[s], 16)
                    for w in range(1, 4):
                        sp.dma_start(vw[to_row:to_row + 64, s, w, :], v_sb[WIN * (w - 1):WIN * (w + 1), s, par, :]).then_inc(vw_ready[s], 16)

            with nc.allow_non_contiguous_dma(reason="small parameters, one per partition"):
                load_raw(0)
                for src, dst in ((rot_tables, rot_base[:, :, :, :]), (window_mask, mask_w[:, :, :]), (causal_mask, mask_c[:, :]),
                                 (eye, ident[:, :]), (eye_bf, ident_b[:, :])):
                    sp.dma_start(dst, src).then_inc(const_in, 16)
                for i, s_ in enumerate((q_scale, k_scale)):
                    src = s_.rearrange("(o l) d -> o l d", o=1).to_broadcast([128, DEPTH, DH])
                    sp.dma_start(qks[:, 2 * i, :, :], src).then_inc(const_in, 16)
                    for a in range(2):
                        sp.dma_start(qks[:, 2 * i + 1, :, a * (DH // 2):(a + 1) * (DH // 2)],
                                     src[:, :, (1 - a) * (DH // 2):(2 - a) * (DH // 2)]).then_inc(const_in, 16)
                for b in range(2):
                    sp.dma_start(xin[:, b], X[b, :, :].rearrange("(t p) d -> p t d", p=128)).then_inc(x_in[b], 16)
                with sp.Fori(1, BATCH // 2) as pair:
                    for j in range(2):
                        b = pair * 2
                        sp.wait_ge(f_norm, b + (j - 1))
                        sp.dma_start(xin[:, j], X[bass.ds(b + j, 1), :, :].rearrange("o (t p) d -> p (o t) d", p=128)).then_inc(x_in[j], 16)
                load_wo(0)
                load_ln(0)
                load_ff(0)
                sp.wait_ge(zeroed, 1)
                windows(0, 0)
                windows(1, 1)
                with sp.Fori(2, 16, 2) as t:
                    windows(t, 0)
                    windows(t + 1, 1)
                with sp.Fori(1, DEPTH) as layer:
                    load_raw(layer)
                    for lo, hi, then in ((-16, 2, load_wo), (2, 6, load_ln), (6, 8, load_ff), (8, 16, None)):
                        with sp.Fori(lo, hi, 2) as t:
                            windows(layer * 32 + t, 0)
                            windows(layer * 32 + t + 1, 1)
                        if then:
                            then(layer)
                with sp.Fori(NTILES - 16, NTILES, 2) as t:
                    windows(t, 0)
                    windows(t + 1, 1)
                sp.wait_ge(wsplit_lo, DEPTH * 6)
                for src, dst in ((Wq, wq_sb[:, 0, :]), (Wk, wq_sb[:, 1, :]), (Wv, wv_sb)):
                    sp.dma_start(dst, src).then_inc(l_w, 16)
                sp.wait_ge(summed, 2 * NUNITS)
                for b in range(2):
                    sp.dma_start(xin[:, b], X[b, :, :].rearrange("(t p) d -> p t d", p=128)).then_inc(l_x[b], 16)

                def store(b, j):
                    sp.wait_ge(l_res, b * TILES + TILES)
                    sp.dma_start(out[bass.ds(b, 1), :, :].rearrange("o (t p) d -> p (o t) d", p=128),
                                 last_o[:, j, :].rearrange("p (t d) -> p t d", t=TILES)).then_inc(l_out[j], 16)

                with sp.Fori(0, BATCH // 2 - 1) as pair:
                    for j in range(2):
                        b = pair * 2
                        store(b + j, j)
                        sp.dma_start(xin[:, j], X[bass.ds(b + (j + 2), 1), :, :].rearrange("o (t p) d -> p (o t) d", p=128)).then_inc(l_x[j], 16)
                for j in range(2):
                    store(BATCH - 2 + j, j)
                for j in range(2):
                    sp.wait_ge(l_out[j], 16 * (BATCH // 2))

        @block.tensor
        def _(pe):
            pe.wait_ge(const_in, CONSTS * 16)
            pe.wait_ge(zeroed, 1)
            def first(b, j, pair):
                pe.wait_ge(f_norm, b + 1)
                wait(pe, f_cp, b - 1)
                for t in range(TILES):
                    m = nc.tensor.transpose(ps[:, T_BANK[j], t * 128:t * 128 + 128], qk[:, j, 0, t * 128:t * 128 + 128], ident[:, :])
                m.then_inc(f_tr, 1)

            pairs(pe, first)

            def project(g, n, kind):
                u, h, t = unit(g, n, 0), half(n, 0), tslot(n, 0)
                bank = ps[:, P_BANK[(3 * n + kind) % 2], :]
                if kind == 0:
                    wait(pe, rotated, 2 * u)
                elif kind == 1:
                    wait(pe, v_copied, u)
                else:
                    wait(pe, rotated, 2 * u + 1)
                lhs = (xh[:, t * 128:t * 128 + 128], xh[:, t * 128:t * 128 + 128], xl[:, t * 128:t * 128 + 128])
                rhs = (chunk(wqkv_hi, kind, h), chunk(wqkv_lo, kind, h), chunk(wqkv_hi, kind, h))
                for i in range(3):
                    m = nc.tensor.matmul(bank, lhs[i], rhs[i], start=i == 0, stop=i == 2)
                m.then_inc(projected, 1)

            def transposes(g, kind, n, source, done):
                t_free(pe, g, kind, n)
                for i in range(4):
                    m = nc.tensor.transpose(ps[:, t_bank(kind, n), i * 128:i * 128 + 128], source[:, i * 128:i * 128 + 128], ident[:, :])
                m.then_inc(done, 1)

            def scores(g, n):
                u, h, s = unit(g, n, T_LAG), half(n, T_LAG), slot(n, T_LAG, 2)
                wait(pe, cq, u + 1)
                wait(pe, ck, u + 1)
                wait(pe, o_copied, u - 1)
                wait(pe, subbed, u)
                first = 0 if tslot(n, T_LAG) == 0 else 1
                for par in range(2):
                    nc.tensor.matmul(ps[:, S_BANK + par, 0:256], ident_b[:, :], mask_w[:, first, :], start=True, stop=False, skip_group_check=True)
                kt = kT[:, h, tslot(n, T_LAG) % 2]
                for hp in range(4):
                    for w in range(4):
                        for par in range(2):
                            rows = slice(64 * par, 64 * par + 64)
                            m = nc.tensor.matmul(ps[WIN * w:WIN * w + WIN, S_BANK + par, hp * 64:hp * 64 + 64],
                                                 qT[rows, s, hp, WIN * w:WIN * w + WIN], kt[rows, hp, WIN * w:WIN * w + 64],
                                                 start=False, stop=True, skip_group_check=True)
                m.then_inc(scored, 1)

            def attend(g, n):
                u, h, s, tile = unit(g, n, P_LAG), half(n, P_LAG), slot(n, P_LAG, 2), tslot(n, P_LAG)
                pairs = (g - 1 if n < P_LAG else g) * 2 + tile // 2
                edge_in, windows_in = pairs * 32 + 32, pairs * 128 + 128
                if not isinstance(windows_in, int):
                    edge_in, windows_in = pe.to_reg(edge_in), pe.to_reg(windows_in)
                pe.wait_ge(zeroed, 1)
                wait(pe, vw_edge[tile % 2], edge_in)
                wait(pe, vw_ready[tile % 2], windows_in)
                wait(pe, cp, u + 1)
                wait(pe, o_copied, u)
                for hp in range(4):
                    for w in range(4):
                        for par in range(2):
                            rows = slice(64 * par, 64 * par + 64)
                            m = nc.tensor.matmul(ps[WIN * w:WIN * w + WIN, S_BANK + par, 256 + hp * 64:320 + hp * 64],
                                                 pT[rows, s, hp, WIN * w:WIN * w + WIN], vw[rows, tile % 2, w, (4 * h + hp) * 64:(4 * h + hp) * 64 + 64],
                                                 start=True, stop=True, skip_group_check=True)
                m.then_inc(attended, 1)

            def tile_of(g, n):
                return g * TILES + (n - WO_LAG) // 2

            def ffn_chunk(part, bank, c, rows):
                cols = slice(part * FF + c * FC, part * FF + c * FC + rows)
                for i, (w, x) in enumerate(((w1_hi, xn_hi), (w1_lo, xn_hi), (w1_hi, xn_lo))):
                    m = nc.tensor.matmul(bank[0:rows, :], w[:, cols], x[:, :], start=i == 0, stop=i == 2)
                m.then_inc(gate_done if part else a_done, 1)

            def body(g, b, layer):
                for n in range(UPB):
                    now, ffn = live(unit(g, n, 0), NUNITS), live(g - 2, BODIES)
                    if now:
                        if n % 2 == 0:
                            wait(pe, xl_ready, g * TILES + n // 2 + 1)
                        if isinstance(b, int) and b == 0 and n < 2:
                            pe.wait_ge(wsplit_lo, layer * 6 + (3 * n + 3))
                        project(g, n, 0)
                    if live(unit(g, n, T_LAG), NUNITS):
                        wait(pe, normed, 2 * unit(g, n, T_LAG) + 1)
                        transposes(g, "q", n, qk[:, slot(n, T_LAG, 4), 0, :], tq)
                    if now:
                        project(g, n, 1)
                    if live(unit(g, n, T_LAG), NUNITS):
                        wait(pe, normed, 2 * unit(g, n, T_LAG) + 2)
                        transposes(g, "k", n, qk[:, slot(n, T_LAG, 4), 1, :], tk)
                    if n == 1 and ffn:
                        wait(pe, xt_normed, g - 1)
                        transposes(g, "lnb", n, xt[:, :, :].rearrange("p t d -> p (t d)"), tlb)
                    if n in (2, 3, 4) and ffn:
                        c = n - 2
                        if c == 0:
                            if not isinstance(b, int) or b == 2:
                                pe.wait_ge(w1_lo_ready, layer + 1)
                            wait(pe, xnl_ready, g - 1)
                            wait(pe, res2, g - 2)
                        wait(pe, a_copied, (g - 2) * NFC + c)
                        ffn_chunk(1, W1B, c, FROWS[c])
                    if n == 6 and ffn:
                        if not isinstance(b, int) or b == 2:
                            pe.wait_ge(ffp_in, (layer + 1) * 160)
                        wait(pe, hid_done, g - 1)
                        for c, rows in enumerate(FROWS):
                            m = nc.tensor.matmul(W1B, w2_sb[0:rows, c, :], hid[0:rows, c, :], start=c == 0, stop=c == NFC - 1)
                        m.then_inc(down_done, 1)
                    if now:
                        project(g, n, 2)
                    if n % 2 == 1 and live(tile_of(g, n), NTILES):
                        T = tile_of(g, n)
                        wait(pe, co, 2 * T + 2)
                        wait(pe, res1, T)
                        if isinstance(b, int) and b == 0 and n == 7:
                            pe.wait_ge(wo_in, (layer + 1) * 16)
                        s = (n - WO_LAG) // 2 % 2
                        for c in range(8):
                            m = nc.tensor.matmul(W0[:, 0:128], wo_sb[:, c, :], oT[:, s, c, :], start=c == 0, stop=c == 7)
                        m.then_inc(wo_done, 1)
                    if live(unit(g, n, O_LAG), NUNITS):
                        wait(pe, o_copied, unit(g, n, O_LAG) + 1)
                        transposes(g, "o", n, o_sb[:, slot(n, O_LAG, 2), :], to)
                    if live(unit(g, n, P_LAG), NUNITS):
                        wait(pe, expd, unit(g, n, P_LAG) + 1)
                        transposes(g, "p", n, prob[:, slot(n, P_LAG, 2), :], tp)
                    if n in (2, 3, 4) and ffn:
                        c = n - 2
                        wait(pe, gate_copied, (g - 2) * NFC + (c + 1))
                        ffn_chunk(0, W1B, c, FROWS[c])
                    if n == 6 and live(g - 1, BODIES):
                        wait(pe, x2_ready, g)
                        transposes(g, "ln", n, x2[:, :], tlf)
                    if live(unit(g, n, T_LAG), NUNITS):
                        scores(g, n)
                    if live(unit(g, n, P_LAG), NUNITS):
                        attend(g, n)

            bodies(pe, body)

            def last(b, j, pair):
                pe.wait_ge(l_norm, b + 1)
                for t in range(TILES):
                    m = nc.tensor.transpose(ps[:, 2, t * 128:t * 128 + 128], xt[:, t, :], ident[:, :])
                m.then_inc(l_tr, 1)
                pe.wait_ge(l_fs, b + 1)
                for t in range(TILES):
                    m = nc.tensor.transpose(ps[:, 3, t * 128:t * 128 + 128], last_f[:, 0, t * 128:t * 128 + 128], ident[:, :])
                m.then_inc(l_ft, 1)
                pe.wait_ge(l_cp, b + 1)
                for i in range(2):
                    nc.tensor.matmul(ps[0:DQ, i, :], wq_sb[:, i, :], xn[:, :], start=True, stop=True).then_inc(l_mm, 1)
                for t in range(TILES):
                    m = nc.tensor.matmul(ps[:, 6, t * 128:t * 128 + 128], xn[:, t * 128:t * 128 + 128], wv_sb[:, :], start=True, stop=True)
                m.then_inc(l_mm, 1)
                pe.wait_ge(l_ev, b * 3 + 3)
                for t in range(TILES):
                    keys = (t + 1) * 128
                    T = b * TILES + t
                    nc.tensor.matmul(ps[:, 4 + t % 2, 0:keys], ident_b[:, :], mask_c[:, SEQ - keys:SEQ], start=True, stop=False, skip_group_check=True)
                    nc.tensor.matmul(ps[:, 4 + t % 2, 0:keys], last_q[:, t * 128:t * 128 + 128], last_k[:, 0:keys], start=False, stop=True, skip_group_check=True).then_inc(l_s, 1)
                    pe.wait_ge(l_ex, T + 1)
                    for c in range(t + 1):
                        m = nc.tensor.transpose(ps[:, 2, c * 128:c * 128 + 128], last_p[:, t % 2, c * 128:c * 128 + 128], ident[:, :])
                    m.then_inc(l_pt, 1)
                    pe.wait_ge(l_pc, T + 1)
                    if t == 0:
                        pe.wait_ge(l_acc, b + 1)
                    else:
                        pe.wait_ge(l_res, T)
                    for c in range(t + 1):
                        m = nc.tensor.matmul(ps[:, 7, 0:128], last_pT[:, t % 2, c * 128:c * 128 + 128], last_v[:, c, :], start=c == 0, stop=c == t)
                    m.then_inc(l_o, 1)

            pe.wait_ge(l_w, 48)
            pairs(pe, last)

        @block.scalar
        def _(act):
            act.preload_act_table(ACT.Exp)
            act.wait_ge(zeroed, 1)
            def first(b, j, pair):
                act.wait_ge(f_tr, b + 1)
                nc.scalar.activation(state(b, 0, SEQ, slice(0, 64)), ps[0:64, T_BANK[j], :], ACT.Copy)
                nc.scalar.activation(state(b, 1, SEQ, slice(64, 128)), ps[64:128, T_BANK[j], :], ACT.Copy).then_inc(f_cp, 1)

            pairs(act, first)

            def high_part(g, b, layer, t):
                if isinstance(layer, int):
                    act.wait_ge(f_cp, BATCH)
                else:
                    act.wait_ge(res2, g - (BATCH - 1))
                wait(act, projected, (g * UPB + 2 * t - UPB + 2) * 3)
                nc.scalar.activation(xh[:, t * 128:t * 128 + 128], state(b, t * 128, 128), ACT.Copy).then_inc(xh_ready, 1)

            def square(g, n, kind):
                u = unit(g, n, 0)
                act.wait_ge(projected, 3 * u + kind + 1)
                wait(act, reduced, 2 * u + kind - 1)
                nc.scalar.activation(sq[:, kind, :], ps[:, P_BANK[(3 * n + kind) % 2], :], ACT.Square).then_inc(squared, 1)

            def body(g, b, layer):
                peeled = isinstance(b, int)
                for n in range(UPB):
                    if peeled and b == 0 and layer is not None and n < 2:
                        if n == 0:
                            act.wait_ge(raw_in, layer * 16 + 16)
                        if not isinstance(layer, int):
                            act.wait_ge(projected, (unit(g, n, 2) + 1) * 3)
                        for kind in range(3):
                            dst, src = chunk(wqkv_hi, kind, n), raw_chunk(kind, n)
                            nc.scalar.activation(view_v(dst) if kind == 2 else dst, src, ACT.Copy).then_inc(wsplit_hi, 1)
                    if live(unit(g, n, 0), NUNITS):
                        if n == 0:
                            high_part(g, b, layer, 0)
                    now, ffn = live(unit(g, n, 0), NUNITS), live(g - 2, BODIES)
                    if now:
                        square(g, n, 0)
                    if live(unit(g, n, T_LAG), NUNITS):
                        u, s = unit(g, n, T_LAG), slot(n, T_LAG, 2)
                        act.wait_ge(tq, u + 1)
                        wait(act, scored, u - 1)
                        nc.scalar.activation(qT[:, s, :, :].rearrange("p a b -> p (a b)"), ps[:, t_bank("q", n), :], ACT.Copy).then_inc(cq, 1)
                    if live(unit(g, n, P_LAG), NUNITS):
                        u, s = unit(g, n, P_LAG), slot(n, P_LAG, 2)
                        act.wait_ge(subbed, u + 1)
                        wait(act, tp, u - 1)
                        wait(act, sumd, u - 1)
                        nc.scalar.activation(prob[:, s, :].rearrange("p (a b c) -> p b a c", a=4, b=2),
                                             dsub[:, s, :].rearrange("p (b a c) -> p b a c", a=4, b=2), ACT.Exp, scale=8.0).then_inc(expd, 1)
                    if now:
                        square(g, n, 1)
                    if live(unit(g, n, T_LAG), NUNITS):
                        u, h, ts = unit(g, n, T_LAG), half(n, T_LAG), tslot(n, T_LAG) % 2
                        src = ps[:, t_bank("k", n), :].rearrange("p (a b) -> p a b", a=4)
                        act.wait_ge(tk, u + 1)
                        wait(act, scored, u - 1)
                        nc.scalar.activation(kT[:, h, ts, :, WIN:], src, ACT.Copy)
                        nc.scalar.activation(kT[:, h, 1 - ts, :, 0:WIN], src[:, :, 128 - WIN:], ACT.Copy).then_inc(ck, 1)
                    if n == 1 and ffn:
                        if not peeled or b == 2:
                            act.wait_ge(lnp_in, (layer + 1) * 32)
                        act.wait_ge(tlb, g - 1)
                        wait(act, xnl_ready, g - 2)
                        nc.scalar.activation(xn[:, :], ps[:, t_bank("lnb", 1), :], ACT.Identity, bias=lnb_sb[:, 0:1], scale=lng_sb[:, 0:1]).then_inc(clb, 1)
                        wait(act, a_done, (g - 2) * NFC)
                        act.wait_ge(clb, g - 1)
                        nc.scalar.activation(xn_hi[:, :], xn[:, :], ACT.Copy).then_inc(xnh_ready, 1)
                    if n in (2, 3, 4) and ffn:
                        c = n - 2
                        rows = FROWS[c]
                        act.wait_ge(gate_done, (g - 2) * NFC + (c + 1))
                        if c == 0:
                            if not peeled or b == 2:
                                act.wait_ge(ffp_in, (layer + 1) * 160)
                            wait(act, hid_done, g - 2)
                        nc.scalar.activation(gate[0:rows, c, :], W1B[0:rows, :], ACT.Identity, bias=b1_sb[0:rows, 1, c:c + 1]).then_inc(gate_copied, 1)
                    if n == 6 and live(g - 1, BODIES):
                        act.wait_ge(res1, g * TILES)
                        wait(act, tlf, g - 1)
                        nc.scalar.activation(x2[:, :], state(prev_batch(b, 1), 0, SEQ), ACT.Copy).then_inc(x2_ready, 1)
                    if now:
                        u, par, ts = unit(g, n, 0), half(n, 0), tslot(n, 0) % 2
                        act.wait_ge(projected, 3 * u + 3)
                        if par == 0:
                            before = g * 2 + n // 4
                            wait(act, vw_ready[ts], before * 128)
                            wait(act, vw_edge[1 - ts], (before + ts) * 32)
                        nc.scalar.activation(v_sb[:, ts, par, :], ps[:, P_BANK[(3 * n + 2) % 2], :], ACT.Copy).then_inc(v_copied, 1)
                        if n % 2 == 1 and n < UPB - 1:
                            high_part(g, b, layer, (n + 1) // 2)
                    if live(unit(g, n, O_LAG), NUNITS):
                        u, h = unit(g, n, O_LAG), half(n, O_LAG)
                        act.wait_ge(to, u + 1)
                        if h == 0:
                            wait(act, wo_done, tile2(g, n) - 1)
                        nc.scalar.activation(oT[:, tslot(n, O_LAG) % 2, 4 * h:4 * h + 4, :].rearrange("p a b -> p (a b)"),
                                             ps[:, t_bank("o", n), :], ACT.Copy).then_inc(co, 1)
                    if live(unit(g, n, P_LAG), NUNITS):
                        u, s = unit(g, n, P_LAG), slot(n, P_LAG, 2)
                        act.wait_ge(tp, u + 1)
                        wait(act, attended, u - 1)
                        nc.scalar.activation(pT[:, s, :, :].rearrange("p a b -> p (a b)"), ps[:, t_bank("p", n), :], ACT.Copy).then_inc(cp, 1)
                    if n == 6 and live(g - 1, BODIES):
                        act.wait_ge(tlf, g)
                        wait(act, tlb, g - 1)
                        nc.scalar.activation(xt[:, :, :].rearrange("p t d -> p (t d)"), ps[:, t_bank("ln", 6), :], ACT.Copy).then_inc(clf, 1)
                    if n == 4 and ffn:
                        act.wait_ge(gate_copied, (g - 2) * NFC + NFC)
                        nc.scalar.activation(gate[:, :, :].rearrange("p a b -> p (a b)"), gate[:, :, :].rearrange("p a b -> p (a b)"), ACT.Gelu).then_inc(gelu_done, 1)
                    if peeled and b == 1 and layer is not None and n == 5:
                        act.wait_ge(w1raw_in, layer * 16 + 16)
                        if not isinstance(layer, int):
                            act.wait_ge(a_done, layer * (BATCH * NFC))
                        nc.scalar.activation(w1_hi[:, :], w1_raw[:, :], ACT.Copy).then_inc(w1_hi_ready, 1)

            def tile2(g, n):
                return g * TILES + (n - O_LAG) // 2

            bodies(act, body)

            def last(b, j, pair):
                act.wait_ge(l_tr, b + 1)
                nc.scalar.activation(xn[:, :], ps[:, 2, :], ACT.Copy).then_inc(l_cp, 1)
                act.wait_ge(l_mm, b * 3 + 1)
                nc.scalar.activation(last_q, ps[0:DQ, 0, :], ACT.Copy).then_inc(l_ev, 1)
                act.wait_ge(l_mm, b * 3 + 2)
                nc.scalar.activation(last_k, ps[0:DQ, 1, :], ACT.Copy).then_inc(l_ev, 1)
                act.wait_ge(l_mm, b * 3 + 3)
                nc.scalar.activation(last_v, ps[:, 6, :].rearrange("p (t d) -> p t d", t=TILES), ACT.Copy).then_inc(l_ev, 1)
                for t in range(TILES):
                    T, keys = b * TILES + t, (t + 1) * 128
                    act.wait_ge(l_ng, T + 1)
                    nc.scalar.activation(last_p[:, t % 2, 0:keys], ps[:, 4 + t % 2, 0:keys], ACT.Exp, bias=smax[:, 1, t:t + 1],
                                         scale=1 / math.sqrt(DQ), accum_out=rsum[:, 0, t:t + 1]).then_inc(l_ex, 1)
                    act.wait_ge(l_pt, T + 1)
                    nc.scalar.activation(last_pT[:, t % 2, 0:keys], ps[:, 2, 0:keys], ACT.Copy).then_inc(l_pc, 1)

            pairs(act, last)

        @block.vector
        def _(dve):
            def rsqrt_step(k, x, y, tmp, done, before):
                if k > 0:
                    dve.wait_ge(done, before + k)
                if k == 0:
                    i = nc.vector.tensor_scalar(tmp.bitcast(I32), x.bitcast(I32), 1, None, ALU.logical_shift_right)
                elif k == 1:
                    i = nc.vector.tensor_scalar(y.bitcast(I32), tmp.bitcast(I32), -1.0, SQRT_MAGIC, ALU.mult, ALU.add)
                elif k % 3 == 2:
                    i = nc.vector.tensor_tensor(tmp, y, y, ALU.mult)
                elif k % 3 == 0:
                    i = nc.vector.scalar_tensor_tensor(tmp, tmp, -0.5, x, ALU.mult, ALU.mult)
                else:
                    i = nc.vector.scalar_tensor_tensor(y, tmp, 1.5, y, ALU.add, ALU.mult)
                i.then_inc(done, 1)

            def ln_statistics(src, s_bn, s_ag, s_out, i):
                wait(dve, s_out, i)
                for t in range(TILES):
                    nc.vector.bn_stats(bst[:, t, :], src[:, t, :]).then_inc(s_bn, 1)
                dve.wait_ge(s_bn, i * TILES + TILES)
                nc.vector.memset(lnv[:, :], 1e-5).then_inc(s_ag, 1)
                for t in range(TILES):
                    nc.vector.bn_aggr(mv[:, t, :], bst[:, t, :]).then_inc(s_ag, 1)
                dve.wait_ge(s_ag, i * 6 + 5)
                nc.vector.tensor_tensor(lnv[:, :], lnv[:, :], mv[:, :, 1], ALU.add).then_inc(s_ag, 1)

            def ln_newton_step(k, s_ag, s_nw, i):
                if k == 0:
                    dve.wait_ge(s_ag, i * 6 + 6)
                rsqrt_step(k, lnv[:, :], lnr[:, :], lnt[:, :], s_nw, i * NEWTON)

            def ln_normalise(src, dst, s_nw, s_out, i):
                dve.wait_ge(s_nw, i * NEWTON + NEWTON)
                for t in range(TILES):
                    m = nc.vector.tensor_scalar(dst[:, t, :], src[:, t, :], mv[:, t, 0:1], lnr[:, t:t + 1], ALU.subtract, ALU.mult)
                m.then_inc(s_out, 1)

            def layer_norm(src, dst, s_bn, s_ag, s_nw, s_out, i, dst_read=None):
                ln_statistics(src, s_bn, s_ag, s_out, i)
                for k in range(NEWTON):
                    ln_newton_step(k, s_ag, s_nw, i)
                if dst_read:
                    wait(dve, dst_read, i - 1)
                ln_normalise(src, dst, s_nw, s_out, i)

            for buf in (kT, v_sb, gate, xs):
                last = nc.vector.memset(buf[:], 0.0)
            last.then_inc(zeroed, 1)
            def first(b, j, pair):
                dve.wait_ge(x_in[j], pair * 16 + 16)
                layer_norm(xin[:, j], qk[:, j, 0, :].rearrange("p (t d) -> p t d", t=TILES), f_bn, f_ag, f_newton, f_norm, b, f_tr)

            pairs(dve, first)

            def rotary(g, n, kind):
                u, s, t = unit(g, n, 0), slot(n, 0, 2), tslot(n, 0)
                x = ps[:, P_BANK[(3 * n + kind) % 2], :]
                dve.wait_ge(squared, 2 * u + kind + 1)
                wait(dve, summed, 2 * (u - 2) + kind + 1)
                cos = rot[:, 2 * kind, t, :].rearrange("p (o d) -> p o d", o=1).to_broadcast([128, 8, DH])
                nc.vector.tensor_tensor(view_v(t1[:, s, kind, :]), view_v(x), cos, ALU.mult)

            def rotary2(g, n, kind):
                s, t = slot(n, 0, 2), tslot(n, 0)
                x = ps[:, P_BANK[(3 * n + kind) % 2], :].rearrange("p (h a d) -> p h a d", a=2, d=DH // 2)[:, :, ::-1, :]
                sin = rot[:, 2 * kind + 1, t, :].rearrange("p (o a d) -> p o a d", o=1, a=2).to_broadcast([128, 8, 2, DH // 2])
                nc.vector.tensor_tensor(t2[:, s, kind, :].rearrange("p (h a d) -> p h a d", a=2, d=DH // 2), x, sin, ALU.mult).then_inc(rotated, 1)

            def sums_of_squares(g, n, kind):
                u, s = unit(g, n, 0), slot(n, 0, 2)
                wait(dve, newton, (u - 1) * NEWTON) if kind == 0 else None
                nc.vector.tensor_reduce(n2[:, s, 8 * kind:8 * kind + 8], view_v(sq[:, kind, :]), AX.X, ALU.add).then_inc(reduced, 1)

            def norm_step(g, n, k):
                u = unit(g, n, 1)
                if live(u, NUNITS):
                    if k == 0:
                        dve.wait_ge(reduced, 2 * u + 2)
                        wait(dve, normed, 2 * (u - 3))
                    rsqrt_step(k, n2[:, slot(n, 1, 2), :], rn[:, slot(n, 1, 4), :], nwt[:, :], newton, u * NEWTON)

            def clamp(g, n):
                u = unit(g, n, 1)
                if live(u, NUNITS):
                    dve.wait_ge(reduced, 2 * u + 2)
                    x = n2[:, slot(n, 1, 2), :]
                    nc.vector.tensor_scalar(x, x, 1e-24, None, ALU.max).then_inc(clamped, 1)
                    dve.wait_ge(clamped, u + 1)

            def body(g, b, layer):
                peeled = isinstance(b, int)
                for n in range(UPB):
                    now = live(unit(g, n, 0), NUNITS)
                    if peeled and b == 0 and layer is not None and n == 0:
                        wait(dve, rotated, g * (2 * UPB))
                        if isinstance(layer, int):
                            dve.wait_ge(const_in, CONSTS * 16)
                        for i in range(4):
                            sc = qks[:, i, bass.ds(layer, 1), :].to_broadcast([128, TILES, DH])
                            m = nc.vector.tensor_tensor(rot[:, i, :, :], rot_base[:, i, :, :], sc, ALU.mult)
                        m.then_inc(rot_ready, 1)
                    if peeled and b == 0 and layer is not None and n < 2:
                        for kind in range(3):
                            dve.wait_ge(wsplit_hi, layer * 6 + (3 * n + kind + 1))
                            lo, hi, raw = chunk(wqkv_lo, kind, n), chunk(wqkv_hi, kind, n).bitcast(F32), raw_chunk(kind, n)
                            if kind == 2:
                                lo, hi = view_v(lo), view_v(hi)
                            nc.vector.tensor_tensor(lo, raw, hi, ALU.subtract).then_inc(wsplit_lo, 1)
                        if n == 0:
                            dve.wait_ge(rot_ready, layer + 1)
                    ffn = live(g - 2, BODIES)
                    clamp(g, n)
                    if now:
                        rotary(g, n, 0)
                    step(g, n, 0)
                    if now:
                        rotary2(g, n, 0)
                    step(g, n, 1)
                    if live(unit(g, n, O_LAG), NUNITS):
                        u, s = unit(g, n, O_LAG), slot(n, O_LAG, 2)
                        dve.wait_ge(attended, u + 1)
                        dve.wait_ge(inverted, u + 1)
                        wait(dve, to, u - 1)
                        O = ps[:, S_BANK:S_BANK + 2, 256:512].rearrange("p b (a c) -> p a b c", a=4)
                        nc.vector.tensor_tensor(o_sb[:, s, :].rearrange("p (a b c) -> p a b c", a=4, b=2), O,
                                                rinv[:, s, :].rearrange("p (a b o) -> p a b o", b=2, o=1).to_broadcast([128, 4, 2, 64]), ALU.mult).then_inc(o_copied, 1)
                    step(g, n, 2)
                    if now:
                        sums_of_squares(g, n, 0)
                    step(g, n, 3)
                    if now:
                        rotary(g, n, 1)
                    step(g, n, 4)
                    if now:
                        rotary2(g, n, 1)
                    step(g, n, 5)
                    if now:
                        sums_of_squares(g, n, 1)
                    step(g, n, 6)
                    if n % 2 == 1 and live(tile1(g, n), NTILES):
                        T, t = tile1(g, n), (n - WO_LAG) // 2 % TILES
                        bb = b if n == 7 else prev_batch(b, 1)
                        dve.wait_ge(wo_done, T + 1)
                        lo, hi = state(bb, t * 128, 128, slice(0, 64)), state(bb, t * 128 + 1, 128, slice(64, 128))
                        nc.vector.tensor_tensor(lo, lo, W0[0:64, 0:128], ALU.add)
                        nc.vector.tensor_tensor(hi, hi, W0[64:128, 0:128], ALU.add).then_inc(res1, 1)
                    step(g, n, 7)
                    if live(unit(g, n, P_LAG), NUNITS):
                        u, s = unit(g, n, P_LAG), slot(n, P_LAG, 2)
                        dve.wait_ge(expd, u + 1)
                        wait(dve, inverted, u - 1)
                        nc.vector.tensor_reduce(rsum[:, s, :], view_v(prob[:, s, :]), AX.X, ALU.add).then_inc(sumd, 1)
                    step(g, n, 8)
                    if n == 5 and ffn:
                        dve.wait_ge(gelu_done, g - 1)
                        dve.wait_ge(a_copied, (g - 2) * NFC + NFC)
                        for c, rows in enumerate(FROWS):
                            m = nc.vector.tensor_tensor(hid[0:rows, c, :], hid[0:rows, c, :], gate[0:rows, c, :], ALU.mult)
                        m.then_inc(hid_done, 1)
                    if peeled and b == 1 and layer is not None and n == 5:
                        dve.wait_ge(w1_hi_ready, layer + 1)
                        nc.vector.tensor_tensor(w1_lo[:, :], w1_raw[:, :], w1_hi[:, :].bitcast(F32), ALU.subtract).then_inc(w1_lo_ready, 1)
                    if n == 6 and ffn:
                        bb = prev_batch(b, 2)
                        dve.wait_ge(down_done, g - 1)
                        lo, hi = state(bb, 0, SEQ, slice(0, 64)), state(bb, 1, SEQ, slice(64, 128))
                        nc.vector.scalar_tensor_tensor(lo, W1B[0:64, :], b2_sb[0:64, 0:1], lo, ALU.add, ALU.add)
                        nc.vector.scalar_tensor_tensor(hi, W1B[64:128, :], b2_sb[64:128, 0:1], hi, ALU.add, ALU.add).then_inc(res2, 1)
                    if n == 7 and live(g - 1, BODIES):
                        dve.wait_ge(clf, g)
                        ln_statistics(xt, bn_done, ag_done, xt_normed, g - 1)
                    step(g, n, 9)
                    if live(unit(g, n, P_LAG), NUNITS):
                        dve.wait_ge(sumd, u + 1)
                        wait(dve, o_copied, u - 1)
                        nc.vector.reciprocal(rinv[:, s, :], rsum[:, s, :]).then_inc(inverted, 1)
                    step(g, n, 10)
                    if n == 0 and ffn:
                        ln_normalise(xt, xt, ln_newton, xt_normed, g - 2)
                    if n == 1 and ffn:
                        dve.wait_ge(xnh_ready, g - 1)
                        nc.vector.tensor_tensor(xn_lo[:, :], xn[:, :], xn_hi[:, :].bitcast(F32), ALU.subtract).then_inc(xnl_ready, 1)
                    if n in (2, 3, 4) and ffn:
                        c = n - 2
                        rows = FROWS[c]
                        dve.wait_ge(a_done, (g - 2) * NFC + (c + 1))
                        if c == 0:
                            if not peeled or b == 2:
                                dve.wait_ge(ffp_in, (layer + 1) * 160)
                            wait(dve, down_done, g - 2)
                        nc.vector.tensor_scalar(hid[0:rows, c, :], W1B[0:rows, :], b1_sb[0:rows, 0, c:c + 1], None, ALU.add).then_inc(a_copied, 1)
                    if live(unit(g, n, T_LAG), NUNITS):
                        u, s = unit(g, n, T_LAG), slot(n, T_LAG, 2)
                        dve.wait_ge(scored, u + 1)
                        if live(unit(g, n, P_LAG), NUNITS):
                            dve.wait_ge(attended, u)
                        S = ps[:, S_BANK:S_BANK + 2, 0:256].rearrange("p b (a c) -> p b a c", a=4)
                        nc.vector.tensor_reduce(smax[:, s, :].rearrange("p (b a) -> p b a", b=2), S, AX.X, ALU.max).then_inc(maxed, 1)
                        dve.wait_ge(maxed, u + 1)
                        wait(dve, expd, u - 1)
                        nc.vector.tensor_tensor(dsub[:, s, :].rearrange("p (b a c) -> p b a c", a=4, b=2), S,
                                                smax[:, s, :].rearrange("p (b a o) -> p b a o", b=2, o=1).to_broadcast([128, 2, 4, 64]), ALU.subtract).then_inc(subbed, 1)

            def step(g, n, k):
                norm_step(g, n, k)
                if n == 0 and live(g - 2, BODIES):
                    ln_newton_step(k, ag_done, ln_newton, g - 2)

            def tile1(g, n):
                return g * TILES + (n - WO_LAG) // 2

            bodies(dve, body)

            def last(b, j, pair):
                dve.wait_ge(l_x[j], pair * 16 + 16)
                wait(dve, l_tr, b)
                layer_norm(xin[:, j], xt, l_bn, l_ag, l_newton, l_norm, b)
                wait(dve, l_ft, b)
                nc.vector.tensor_copy(last_f[0:64, 0, :], state(b, 0, SEQ, slice(0, 64)))
                nc.vector.tensor_copy(last_f[64:128, 0, :], state(b, 1, SEQ, slice(64, 128))).then_inc(l_fs, 1)
                dve.wait_ge(l_ft, b + 1)
                nc.vector.tensor_tensor(last_acc[:, 0, :], ps[:, 3, :], xin[:, j].rearrange("p t d -> p (t d)"), ALU.add).then_inc(l_acc, 1)
                for t in range(TILES):
                    T, keys = b * TILES + t, (t + 1) * 128
                    dve.wait_ge(l_s, T + 1)
                    nc.vector.tensor_reduce(smax[:, 0, t:t + 1], ps[:, 4 + t % 2, 0:keys], AX.X, ALU.max).then_inc(l_mx, 1)
                    dve.wait_ge(l_mx, T + 1)
                    nc.vector.tensor_scalar(smax[:, 1, t:t + 1], smax[:, 0, t:t + 1], -1 / math.sqrt(DQ), None, ALU.mult).then_inc(l_ng, 1)
                    dve.wait_ge(l_ex, T + 1)
                    nc.vector.reciprocal(rinv[:, 0, t:t + 1], rsum[:, 0, t:t + 1]).then_inc(l_iv, 1)
                    dve.wait_ge(l_iv, T + 1)
                    dve.wait_ge(l_o, T + 1)
                    dve.wait_ge(l_acc, b + 1)
                    if t == 0:
                        wait(dve, l_out[j], pair * 16)
                    nc.vector.scalar_tensor_tensor(last_o[:, j, t * 128:t * 128 + 128], ps[:, 7, 0:128], rinv[:, 0, t:t + 1],
                                                   last_acc[:, 0, t * 128:t * 128 + 128], ALU.mult, ALU.add).then_inc(l_res, 1)

            pairs(dve, last)

        @block.gpsimd
        def _(pool):
            def low_part(g, b, t):
                pool.wait_ge(xh_ready, g * TILES + (t + 1))
                nc.gpsimd.tensor_tensor(xl[:, t * 128:t * 128 + 128], state(b, t * 128, 128), xh[:, t * 128:t * 128 + 128].bitcast(F32), ALU.subtract).then_inc(xl_ready, 1)

            def add(g, n, kind):
                u, s = unit(g, n, 0), slot(n, 0, 2)
                pool.wait_ge(rotated, 2 * u + kind + 1)
                wait(pool, tk if kind else tq, u - 3)
                nc.gpsimd.tensor_tensor(qk[:, slot(n, 0, 4), kind, :], t1[:, s, kind, :], t2[:, s, kind, :], ALU.add).then_inc(summed, 1)

            def mul(g, n, kind):
                u, s = unit(g, n, 2), slot(n, 2, 4)
                pool.wait_ge(newton, (u + 1) * NEWTON)
                pool.wait_ge(summed, 2 * u + kind + 1)
                x = view_v(qk[:, s, kind, :])
                r = rn[:, s, 8 * kind:8 * kind + 8].rearrange("p (h o) -> p h o", o=1).to_broadcast([128, 8, DH])
                nc.gpsimd.tensor_tensor(x, x, r, ALU.mult).then_inc(normed, 1)

            def body(g, b, layer):
                for n in range(UPB):
                    if n == 0 and live(unit(g, n, 0), NUNITS):
                        low_part(g, b, 0)
                    if live(unit(g, n, 2), NUNITS):
                        mul(g, n, 0)
                        mul(g, n, 1)
                    if live(unit(g, n, 0), NUNITS):
                        add(g, n, 0)
                        if n % 2 == 1 and n < UPB - 1:
                            low_part(g, b, (n + 1) // 2)
                        add(g, n, 1)

            bodies(pool, body)


_INS = ["L0_attn_X", "L0_attn_Wq", "L0_attn_Wk", "L0_attn_Wv", "L0_ffn_Wqkv", "L0_ffn_q_scale", "L0_ffn_k_scale",
        "L0_ffn_Wo", "L0_ffn_ln_g", "L0_ffn_ln_b", "L0_ffn_W1", "L0_ffn_b1", "L0_ffn_W2", "L0_ffn_b2"]


def constants():
    f = np.float32
    halfd = np.arange(0, DH, 2, dtype=f)
    inv_freq = (f(1.0) / f(10000.0) ** (halfd / f(DH))).astype(f)
    tok = np.arange(SEQ, dtype=f)
    freqs = np.concatenate([tok[:, None] * inv_freq[None, :]] * 2, -1).astype(f)
    base = ((halfd + f(0.4 * DH)) / f(1.4 * DH)).astype(f)
    power = ((tok - f(SEQ // 2)) / f(WIN // 2)).astype(f)
    scale = np.concatenate([(base[None, :] ** power[:, None]).astype(f)] * 2, -1)
    cos, sin = np.cos(freqs), np.sin(freqs)
    sign = np.where(np.arange(DH) < DH // 2, f(-1), f(1))
    tables = np.stack([cos * scale, sin * scale * sign, cos / scale, sin / scale * sign]).astype(f)
    tables = tables.reshape(4, TILES, 128, DH).transpose(2, 0, 1, 3)
    q, c = np.arange(128)[:, None], np.arange(2 * WIN)[None, :]
    ok = (c >= q % WIN) & (c <= q % WIN + WIN)
    first = ok & ((q >= WIN) | (c >= WIN))
    window = np.where(np.stack([first, ok], 1), 0.0, MASKED)
    window = np.tile(window[:, :, None, :], (1, 1, 4, 1)).reshape(128, 2, 256)
    causal = np.zeros((128, SEQ))
    causal[:, SEQ - 128:] = np.where(np.arange(128)[None, :] <= q, 0.0, MASKED)
    bf = mybir.dt.np(BF16)
    return {"rot_tables": np.ascontiguousarray(tables), "window_mask": window.astype(bf), "causal_mask": causal.astype(bf),
            "eye": np.eye(128, dtype=f), "eye_bf": np.eye(128).astype(bf)}


def kernel(**inputs):
    import concourse.bacc as bacc
    from concourse.bass_utils import run_bass_kernel_spmd

    nc = bacc.Bacc("TRN2", target_bir_lowering=False, num_devices=1)
    arrays = {n: np.ascontiguousarray(inputs[n]) for n in _INS}
    arrays.update(constants())
    args = [nc.dram_tensor(n, a.shape, mybir.dt.from_np(a.dtype), kind="ExternalInput").ap() for n, a in arrays.items()]
    out = nc.dram_tensor("out", (BATCH, SEQ, DIM), F32, kind="ExternalOutput").ap()
    build(nc, *args, out)
    r = run_bass_kernel_spmd(nc, [arrays], core_ids=[0])
    return r.results[0]["out"]
```

```python
import math
from contextlib import ExitStack

import concourse.bass as bass
import numpy as np
from concourse import mybir

F32, F32R, BF16, I32 = mybir.dt.float32, mybir.dt.float32r, mybir.dt.bfloat16, mybir.dt.int32
ACT, ALU, AX = mybir.ActivationFunctionType, mybir.AluOpType, mybir.AxisListType

BATCH, SEQ, DIM = 8, 512, 128
DEPTH, HEADS, DH, WIN = 6, 16, 64, 32
INNER = HEADS * DH
FF = 341
FC = 114
NFC = 3
FROWS = [FC, FC, FF - 2 * FC]
TILES = SEQ // 128
UPB = 2 * TILES
BODIES = DEPTH * BATCH
NUNITS, NTILES = BODIES * UPB, BODIES * TILES
SW = SEQ + 2
DQ = 64
SQRT_MAGIC = float(0x5F3759DF)
NEWTON = 11
MASKED = -1e30
T_LAG, P_LAG, O_LAG, WO_LAG = 3, 4, 5, 7


def build(nc, X, Wq, Wk, Wv, Wqkv, q_scale, k_scale, Wo, ln_g, ln_b, W1, b1, W2, b2,
          rot_tables, window_mask, causal_mask, eye, eye_bf, out):
    ctx = ExitStack()
    with ctx:
        def sb(name, shape, dt=F32):
            return ctx.enter_context(nc.sbuf_tensor(name, shape, dt))

        def sem(name):
            return ctx.enter_context(nc.semaphore(name))

        xs = sb("xs", [128, BATCH * SW])
        wqkv_raw = sb("wqkv_raw", [128, 3 * INNER])
        wqkv_hi = sb("wqkv_hi", [128, 3 * INNER], F32R)
        wqkv_lo = sb("wqkv_lo", [128, 3 * INNER], F32R)
        wo_sb = sb("wo_sb", [128, HEADS // 2, DIM])
        w1_raw = sb("w1_raw", [128, 2 * FF])
        w1_hi = sb("w1_hi", [128, 2 * FF], F32R)
        w1_lo = sb("w1_lo", [128, 2 * FF], F32R)
        w2_sb = sb("w2_sb", [FC, NFC, DIM])
        b1_sb = sb("b1_sb", [FC, 2, NFC])
        b2_sb = sb("b2_sb", [128, 1])
        lng_sb = sb("lng_sb", [128, 1])
        lnb_sb = sb("lnb_sb", [128, 1])
        rot_base = sb("rot_base", [128, 4, TILES, DH])
        rot = sb("rot", [128, 4, TILES, DH])
        qks = sb("qks", [128, 4, DEPTH, DH])
        mask_w = sb("mask_w", [128, 2, 256], BF16)
        mask_c = sb("mask_c", [128, SEQ], BF16)
        ident = sb("ident", [128, 128])
        ident_b = sb("ident_b", [128, 128], BF16)
        xh = sb("xh", [128, SEQ], F32R)
        xl = sb("xl", [128, SEQ], F32R)
        sq = sb("sq", [128, 2, 512])
        t1 = sb("t1", [128, 2, 2, 512])
        t2 = sb("t2", [128, 2, 2, 512])
        qk = sb("qk", [128, 4, 2, 512])
        n2 = sb("n2", [128, 2, 16])
        nwt = sb("nwt", [128, 16])
        rn = sb("rn", [128, 4, 16])
        qT = sb("qT", [128, 2, 4, 128])
        kT = sb("kT", [128, 2, 2, 4, WIN + 128])
        smax = sb("smax", [128, 2, 8])
        dsub = sb("dsub", [128, 2, 512])
        prob = sb("prob", [128, 2, 512])
        rsum = sb("rsum", [128, 2, 8])
        rinv = sb("rinv", [128, 2, 8])
        pT = sb("pT", [128, 2, 4, 128])
        v_sb = sb("v_sb", [128, 2, 2, 512])
        vw = sb("vw", [128, 2, 4, 512])
        o_sb = sb("o_sb", [128, 2, 512])
        oT = sb("oT", [128, 2, 8, 128])
        x2 = sb("x2", [128, SEQ])
        xt = sb("xt", [128, TILES, 128])
        bst = sb("bst", [128, TILES, 6])
        mv = sb("mv", [128, TILES, 2])
        lnt = sb("lnt", [128, TILES])
        lnr = sb("lnr", [128, TILES])
        lnv = sb("lnv", [128, TILES])
        xn = sb("xn", [128, SEQ])
        xn_hi = sb("xn_hi", [128, SEQ], F32R)
        xn_lo = sb("xn_lo", [128, SEQ], F32R)
        gate = sb("gate", [FC, NFC, SEQ])
        hid = sb("hid", [FC, NFC, SEQ])
        xin = t1[:, :, :, :].rearrange("p a b (c d) -> p (a b) c d", c=TILES)
        wq_sb = wqkv_raw[:, 0:2 * DQ].rearrange("p (a d) -> p a d", a=2)
        wv_sb = wqkv_raw[:, 2 * DQ:2 * DQ + DIM]
        last_q, last_k = qk[0:DQ, 0, :, :], qk[0:DQ, 1, :, :]
        last_v = qk[:, 2, :, :].rearrange("p j (t d) -> p j t d", t=TILES)
        last_p, last_pT = qk[:, 3, :, :], dsub
        last_f = x2
        last_acc = t2[:, 0, :, :]
        last_o = o_sb

        ps = ctx.enter_context(nc.psum_tensor("ps", [128, 8, 512], F32))
        P_BANK, T_BANK, S_BANK, W0, W1B = (0, 1), (2, 3), 4, ps[:, 6, :], ps[:, 7, :]

        projected, squared, rotated, reduced = sem("projected"), sem("squared"), sem("rotated"), sem("reduced")
        qk_copied, cos_done = sem("qk_copied"), sem("cos_done")
        v_copied, summed, newton, normed = sem("v_copied"), sem("summed"), sem("newton"), sem("normed")
        xh_ready, xl_ready = sem("xh_ready"), sem("xl_ready")
        tq, tk, tp, to, tlf, tlb = (sem(f"transposed_{x}") for x in ("q", "k", "p", "o", "ln", "lnb"))
        cq, ck, cp, co, clf, clb = (sem(f"copied_{x}") for x in ("q", "k", "p", "o", "ln", "lnb"))
        scored, maxed, subbed, expd = sem("scored"), sem("maxed"), sem("subbed"), sem("expd")
        sumd, inverted, attended, o_copied = sem("sumd"), sem("inverted"), sem("attended"), sem("o_copied")
        clamped = sem("clamped")
        vw_edge, vw_ready = [sem(f"vw_edge{s}") for s in range(2)], [sem(f"vw_ready{s}") for s in range(2)]
        wo_done, res1 = sem("wo_done"), sem("res1")
        x2_ready, bn_done, ag_done, ln_newton, xt_normed = sem("x2_ready"), sem("bn_done"), sem("ag_done"), sem("ln_newton"), sem("xt_normed")
        xnh_ready, xnl_ready = sem("xnh_ready"), sem("xnl_ready")
        gate_done, gate_copied, a_done, a_copied = sem("gate_done"), sem("gate_copied"), sem("a_done"), sem("a_copied")
        gelu_done, hid_done, down_done, res2 = sem("gelu_done"), sem("hid_done"), sem("down_done"), sem("res2")
        raw_in, wsplit_hi, wsplit_lo, rot_ready = sem("raw_in"), sem("wsplit_hi"), sem("wsplit_lo"), sem("rot_ready")
        w1raw_in, w1_hi_ready, w1_lo_ready = sem("w1raw_in"), sem("w1_hi_ready"), sem("w1_lo_ready")
        wo_in, lnp_in, ffp_in, const_in, zeroed = sem("wo_in"), sem("lnp_in"), sem("ffp_in"), sem("const_in"), sem("zeroed")
        eye_in = sem("eye_in")
        x_in = [sem(f"first_x{j}") for j in range(2)]
        f_bn, f_ag, f_newton, f_norm, f_tr, f_cp = (sem(f"first_{x}") for x in ("bn", "ag", "newton", "norm", "tr", "cp"))
        l_x, l_out = [sem(f"last_x{j}") for j in range(2)], [sem(f"last_out{j}") for j in range(2)]
        l_bn, l_ag, l_newton, l_norm, l_tr, l_cp = (sem(f"last_{x}") for x in ("bn", "ag", "newton", "norm", "tr", "cp"))
        l_w = sem("last_w")
        l_mm, l_ev, l_fs, l_ft, l_s, l_mx, l_ng, l_ex, l_iv, l_pt, l_pc, l_o, l_acc, l_res = (
            sem(f"last_{x}") for x in ("mm", "ev", "fs", "ft", "s", "mx", "ng", "ex", "iv", "pt", "pc", "o", "acc", "res"))

        CONSTS = 10

        def wait(e, s, value):
            if not isinstance(value, int) or value > 0:
                e.wait_ge(s, value)

        def at_most(value, total):
            return min(value, total) if isinstance(value, int) else value

        def live(i, total):
            return not isinstance(i, int) or 0 <= i < total

        def bodies(e, body):
            for b in range(3):
                body(b, b, 0)
            with e.Fori(3, BATCH) as b:
                body(b, b, 0)
            with e.Fori(1, DEPTH) as layer:
                body(layer * BATCH, 0, layer)
                body(layer * BATCH + 1, 1, layer)
                with e.Fori(2, BATCH) as b:
                    body(layer * BATCH + b, b, layer)
            body(BODIES, 0, None)
            body(BODIES + 1, 1, None)

        def last_batches(e, body):
            for b in range(2):
                body(b, b, b // 2)
            with e.Fori(1, BATCH // 2 - 1) as pair:
                for j in range(2):
                    body(pair * 2 + j, j, pair)
            for b in range(BATCH - 2, BATCH + 1):
                body(b, b % 2, b // 2)

        def pairs(e, body):
            for j in range(2):
                body(j, j, 0)
            with e.Fori(1, BATCH // 2) as pair:
                for j in range(2):
                    body(pair * 2 + j, j, pair)

        def unit(g, n, lag):
            return g * UPB + (n - lag)

        def slot(n, lag, size):
            return (n - lag) % size

        def half(n, lag):
            return (n - lag) % 2

        def tslot(n, lag):
            return (n - lag) % UPB // 2

        T_USES = []
        for n in range(UPB):
            T_USES += [("q", n), ("k", n), ("p", n), ("o", n)]
            if n == 1:
                T_USES.append(("lnb", 1))
            if n == 6:
                T_USES.append(("ln", 6))
        T_LAGS = {"q": T_LAG, "k": T_LAG, "p": P_LAG, "o": O_LAG}
        T_COPIED = {"q": cq, "k": ck, "p": cp, "o": co, "ln": clf, "lnb": clb}

        def t_bank(kind, n):
            return T_BANK[T_USES.index((kind, n)) % 2]

        def t_free(e, g, kind, n):
            i = T_USES.index((kind, n)) - 2
            k2, n2_ = T_USES[i % len(T_USES)]
            g2 = g if i >= 0 else g - 1
            if k2 == "ln":
                wait(e, clf, at_most(g2, BODIES))
            elif k2 == "lnb":
                wait(e, clb, g2 - 1)
            else:
                wait(e, T_COPIED[k2], at_most(unit(g2, n2_, T_LAGS[k2]) + 1, NUNITS))

        def prev_batch(b, k):
            return (b - k) % BATCH if isinstance(b, int) else b - k

        def state(b, lo, width, part=slice(0, 128)):
            return xs[part, bass.ds(b * SW + lo, width)]

        def raw_chunk(kind, h):
            w = wqkv_raw[:, kind * INNER:(kind + 1) * INNER]
            if kind < 2:
                return w[:, h * 512:h * 512 + 512]
            return w.rearrange("p (a b d) -> p b a d", b=2, d=DH)[:, h]

        def chunk(w, kind, h):
            return w[:, (2 * kind + h) * 512:(2 * kind + h) * 512 + 512]

        def view_v(c):
            return c.rearrange("p (a d) -> p a d", d=DH)

        block = ctx.enter_context(nc.Block())

        @block.sync
        def _(sp):
            def load_raw(layer):
                if not isinstance(layer, int):
                    sp.wait_ge(wsplit_lo, layer * 6)
                    sp.wait_ge(w1_lo_ready, layer)
                sp.dma_start(wqkv_raw[:, :], Wqkv[bass.ds(layer, 1), :, :].rearrange("l p n -> p (l n)")).then_inc(raw_in, 16)
                sp.dma_start(w1_raw[:, :], W1[bass.ds(layer, 1), :, :].rearrange("l p n -> p (l n)")).then_inc(w1raw_in, 16)

            def load_wo(layer):
                if not isinstance(layer, int):
                    sp.wait_ge(wo_done, layer * (BATCH * TILES))
                sp.dma_start(wo_sb[:, :, :], Wo[bass.ds(layer, 1), :, :].rearrange("l (c p) n -> p (l c) n", p=128)).then_inc(wo_in, 16)

            def load_ln(layer):
                if not isinstance(layer, int):
                    sp.wait_ge(clb, layer * BATCH)
                sp.dma_start(lng_sb[:, :], ln_g[bass.ds(layer, 1), :].rearrange("l p -> p l")).then_inc(lnp_in, 16)
                sp.dma_start(lnb_sb[:, :], ln_b[bass.ds(layer, 1), :].rearrange("l p -> p l")).then_inc(lnp_in, 16)

            def load_ff(layer):
                if not isinstance(layer, int):
                    sp.wait_ge(res2, layer * BATCH)
                for c, rows in enumerate(FROWS):
                    sp.dma_start(w2_sb[0:rows, c, :], W2[bass.ds(layer, 1), c * FC:c * FC + rows, :].rearrange("l p n -> p (l n)")).then_inc(ffp_in, 16)
                    for a in range(2):
                        src = b1[bass.ds(layer, 1), a * FF + c * FC:a * FF + c * FC + rows]
                        sp.dma_start(b1_sb[0:rows, a, c:c + 1], src.rearrange("l p -> p l")).then_inc(ffp_in, 16)
                sp.dma_start(b2_sb[:, :], b2[bass.ds(layer, 1), :].rearrange("l p -> p l")).then_inc(ffp_in, 16)

            def windows(tile, s):
                copied, used = tile * 2 + 2, tile * 2 - 2
                if not isinstance(tile, int):
                    copied, used = sp.to_reg(copied), sp.to_reg(used)
                sp.wait_ge(v_copied, copied)
                wait(sp, attended, used)
                for par in range(2):
                    sp.dma_start(vw[par * 64:par * 64 + WIN, s, 0, :], v_sb[96:128, 1 - s, par, :]).then_inc(vw_edge[s], 16)
                for par in range(2):
                    to_row = par * 64
                    sp.dma_start(vw[to_row + WIN:to_row + 64, s, 0, :], v_sb[0:WIN, s, par, :]).then_inc(vw_ready[s], 16)
                    for w in range(1, 4):
                        sp.dma_start(vw[to_row:to_row + 64, s, w, :], v_sb[WIN * (w - 1):WIN * (w + 1), s, par, :]).then_inc(vw_ready[s], 16)

            with nc.allow_non_contiguous_dma(reason="small parameters, one per partition"):
                for b in range(2):
                    sp.dma_start(xin[:, b], X[b, :, :].rearrange("(t p) d -> p t d", p=128)).then_inc(x_in[b], 16)
                sp.dma_start(ident[:, :], eye).then_inc(eye_in, 16)
                load_raw(0)
                for src, dst in ((rot_tables, rot_base[:, :, :, :]), (window_mask, mask_w[:, :, :]), (causal_mask, mask_c[:, :]),
                                 (eye_bf, ident_b[:, :])):
                    sp.dma_start(dst, src).then_inc(const_in, 16)
                for i, s_ in enumerate((q_scale, k_scale)):
                    src = s_.rearrange("(o l) d -> o l d", o=1).to_broadcast([128, DEPTH, DH])
                    sp.dma_start(qks[:, 2 * i, :, :], src).then_inc(const_in, 16)
                    for a in range(2):
                        sp.dma_start(qks[:, 2 * i + 1, :, a * (DH // 2):(a + 1) * (DH // 2)],
                                     src[:, :, (1 - a) * (DH // 2):(2 - a) * (DH // 2)]).then_inc(const_in, 16)
                with sp.Fori(1, BATCH // 2) as pair:
                    for j in range(2):
                        b = pair * 2
                        sp.wait_ge(f_norm, b + (j - 1))
                        sp.dma_start(xin[:, j], X[bass.ds(b + j, 1), :, :].rearrange("o (t p) d -> p (o t) d", p=128)).then_inc(x_in[j], 16)
                load_wo(0)
                load_ln(0)
                load_ff(0)
                sp.wait_ge(zeroed, 1)
                windows(0, 0)
                windows(1, 1)
                with sp.Fori(2, 16, 2) as t:
                    windows(t, 0)
                    windows(t + 1, 1)
                with sp.Fori(1, DEPTH) as layer:
                    load_raw(layer)
                    for lo, hi, then in ((-16, 2, load_wo), (2, 6, load_ln), (6, 8, load_ff), (8, 16, None)):
                        with sp.Fori(lo, hi, 2) as t:
                            windows(layer * 32 + t, 0)
                            windows(layer * 32 + t + 1, 1)
                        if then:
                            then(layer)
                with sp.Fori(NTILES - 16, NTILES, 2) as t:
                    windows(t, 0)
                    windows(t + 1, 1)
                sp.wait_ge(wsplit_lo, DEPTH * 6)
                for src, dst in ((Wq, wq_sb[:, 0, :]), (Wk, wq_sb[:, 1, :]), (Wv, wv_sb)):
                    sp.dma_start(dst, src).then_inc(l_w, 16)
                sp.wait_ge(summed, 2 * NUNITS)
                for b in range(2):
                    sp.dma_start(xin[:, b], X[b, :, :].rearrange("(t p) d -> p t d", p=128)).then_inc(l_x[b], 16)

                def load(b, j):
                    sp.wait_ge(l_acc, b - 1)
                    sp.dma_start(xin[:, j], X[bass.ds(b, 1), :, :].rearrange("o (t p) d -> p (o t) d", p=128)).then_inc(l_x[j], 16)

                def store(b, j):
                    sp.wait_ge(l_res, b * TILES + TILES)
                    sp.dma_start(out[bass.ds(b, 1), :, :].rearrange("o (t p) d -> p (o t) d", p=128),
                                 last_o[:, j, :].rearrange("p (t d) -> p t d", t=TILES)).then_inc(l_out[j], 16)

                load(2, 0)
                load(3, 1)
                with sp.Fori(0, BATCH // 2 - 2) as pair:
                    for j in range(2):
                        store(pair * 2 + j, j)
                        load(pair * 2 + (j + 4), j)
                for b in range(BATCH - 4, BATCH):
                    store(b, b % 2)
                for j in range(2):
                    sp.wait_ge(l_out[j], 16 * (BATCH // 2))

        @block.tensor
        def _(pe):
            pe.wait_ge(eye_in, 16)
            def first(b, j, pair):
                pe.wait_ge(f_norm, b + 1)
                wait(pe, f_cp, b - 1)
                for t in range(TILES):
                    m = nc.tensor.transpose(ps[:, T_BANK[j], t * 128:t * 128 + 128], qk[:, j, 0, t * 128:t * 128 + 128], ident[:, :])
                m.then_inc(f_tr, 1)

            pairs(pe, first)
            pe.wait_ge(const_in, CONSTS * 16)
            pe.wait_ge(zeroed, 1)

            def project(g, b, layer, n, kind):
                u, h, t = unit(g, n, 0), half(n, 0), tslot(n, 0)
                bank = ps[:, P_BANK[(3 * n + kind) % 2], :]
                if isinstance(b, int) and b == 0 and n < 2:
                    pe.wait_ge(wsplit_lo, layer * 6 + (3 * n + kind + 1))
                if kind == 0:
                    wait(pe, rotated, 2 * u)
                elif kind == 1:
                    wait(pe, v_copied, u)
                else:
                    wait(pe, rotated, 2 * u + 1)
                lhs = (xh[:, t * 128:t * 128 + 128], xh[:, t * 128:t * 128 + 128], xl[:, t * 128:t * 128 + 128])
                rhs = (chunk(wqkv_hi, kind, h), chunk(wqkv_lo, kind, h), chunk(wqkv_hi, kind, h))
                for i in range(3):
                    m = nc.tensor.matmul(bank, lhs[i], rhs[i], start=i == 0, stop=i == 2)
                m.then_inc(projected, 1)

            def transposes(g, kind, n, source, done):
                t_free(pe, g, kind, n)
                for i in range(4):
                    m = nc.tensor.transpose(ps[:, t_bank(kind, n), i * 128:i * 128 + 128], source[:, i * 128:i * 128 + 128], ident[:, :])
                m.then_inc(done, 1)

            def scores(g, n):
                u, h, s = unit(g, n, T_LAG), half(n, T_LAG), slot(n, T_LAG, 2)
                wait(pe, cq, u + 1)
                wait(pe, ck, u + 1)
                wait(pe, o_copied, u - 1)
                wait(pe, subbed, u)
                first = 0 if tslot(n, T_LAG) == 0 else 1
                for par in range(2):
                    nc.tensor.matmul(ps[:, S_BANK + par, 0:256], ident_b[:, :], mask_w[:, first, :], start=True, stop=False, skip_group_check=True)
                kt = kT[:, h, tslot(n, T_LAG) % 2]
                for hp in range(4):
                    for w in range(4):
                        for par in range(2):
                            rows = slice(64 * par, 64 * par + 64)
                            m = nc.tensor.matmul(ps[WIN * w:WIN * w + WIN, S_BANK + par, hp * 64:hp * 64 + 64],
                                                 qT[rows, s, hp, WIN * w:WIN * w + WIN], kt[rows, hp, WIN * w:WIN * w + 64],
                                                 start=False, stop=True, skip_group_check=True)
                m.then_inc(scored, 1)

            def attend(g, n):
                u, h, s, tile = unit(g, n, P_LAG), half(n, P_LAG), slot(n, P_LAG, 2), tslot(n, P_LAG)
                pairs = (g - 1 if n < P_LAG else g) * 2 + tile // 2
                edge_in, windows_in = pairs * 32 + 32, pairs * 128 + 128
                if not isinstance(windows_in, int):
                    edge_in, windows_in = pe.to_reg(edge_in), pe.to_reg(windows_in)
                pe.wait_ge(zeroed, 1)
                wait(pe, vw_edge[tile % 2], edge_in)
                wait(pe, vw_ready[tile % 2], windows_in)
                wait(pe, cp, u + 1)
                wait(pe, o_copied, u)
                for hp in range(4):
                    for w in range(4):
                        for par in range(2):
                            rows = slice(64 * par, 64 * par + 64)
                            m = nc.tensor.matmul(ps[WIN * w:WIN * w + WIN, S_BANK + par, 256 + hp * 64:320 + hp * 64],
                                                 pT[rows, s, hp, WIN * w:WIN * w + WIN], vw[rows, tile % 2, w, (4 * h + hp) * 64:(4 * h + hp) * 64 + 64],
                                                 start=True, stop=True, skip_group_check=True)
                m.then_inc(attended, 1)

            def tile_of(g, n):
                return g * TILES + (n - WO_LAG) // 2

            def ffn_chunk(part, bank, c, rows):
                cols = slice(part * FF + c * FC, part * FF + c * FC + rows)
                for i, (w, x) in enumerate(((w1_hi, xn_hi), (w1_lo, xn_hi), (w1_hi, xn_lo))):
                    m = nc.tensor.matmul(bank[0:rows, :], w[:, cols], x[:, :], start=i == 0, stop=i == 2)
                m.then_inc(gate_done if part else a_done, 1)

            def body(g, b, layer):
                for n in range(UPB):
                    now, ffn = live(unit(g, n, 0), NUNITS), live(g - 2, BODIES)
                    if now:
                        if n % 2 == 0:
                            wait(pe, xl_ready, g * TILES + n // 2 + 1)
                        project(g, b, layer, n, 0)
                    if live(unit(g, n, T_LAG), NUNITS):
                        wait(pe, normed, 2 * unit(g, n, T_LAG) + 1)
                        transposes(g, "q", n, qk[:, slot(n, T_LAG, 4), 0, :], tq)
                    if now:
                        project(g, b, layer, n, 1)
                    if live(unit(g, n, T_LAG), NUNITS):
                        wait(pe, normed, 2 * unit(g, n, T_LAG) + 2)
                        transposes(g, "k", n, qk[:, slot(n, T_LAG, 4), 1, :], tk)
                    if n % 2 == 1 and live(tile_of(g, n), NTILES):
                        T = tile_of(g, n)
                        wait(pe, co, 2 * T + 2)
                        wait(pe, res1, T)
                        if isinstance(b, int) and b == 0 and n == 7:
                            pe.wait_ge(wo_in, (layer + 1) * 16)
                        s = (n - WO_LAG) // 2 % 2
                        for c in range(8):
                            m = nc.tensor.matmul(W0[:, 0:128], wo_sb[:, c, :], oT[:, s, c, :], start=c == 0, stop=c == 7)
                        m.then_inc(wo_done, 1)
                    if n in (2, 3, 4) and ffn:
                        c = n - 2
                        if c == 0:
                            if not isinstance(b, int) or b == 2:
                                pe.wait_ge(w1_lo_ready, layer + 1)
                            wait(pe, xnl_ready, g - 1)
                            wait(pe, res2, g - 2)
                        wait(pe, a_copied, (g - 2) * NFC + c)
                        ffn_chunk(1, W1B, c, FROWS[c])
                    if n == 6 and ffn:
                        if not isinstance(b, int) or b == 2:
                            pe.wait_ge(ffp_in, (layer + 1) * 160)
                        wait(pe, hid_done, g - 1)
                        for c, rows in enumerate(FROWS):
                            m = nc.tensor.matmul(W1B, w2_sb[0:rows, c, :], hid[0:rows, c, :], start=c == 0, stop=c == NFC - 1)
                        m.then_inc(down_done, 1)
                    if live(unit(g, n, P_LAG), NUNITS):
                        wait(pe, expd, unit(g, n, P_LAG) + 1)
                        transposes(g, "p", n, prob[:, slot(n, P_LAG, 2), :], tp)
                    if now:
                        project(g, b, layer, n, 2)
                    if live(unit(g, n, O_LAG), NUNITS):
                        wait(pe, o_copied, unit(g, n, O_LAG) + 1)
                        transposes(g, "o", n, o_sb[:, slot(n, O_LAG, 2), :], to)
                    if n == 1 and ffn:
                        wait(pe, xt_normed, g - 1)
                        transposes(g, "lnb", n, xt[:, :, :].rearrange("p t d -> p (t d)"), tlb)
                    if n in (2, 3, 4) and ffn:
                        c = n - 2
                        wait(pe, gate_copied, (g - 2) * NFC + (c + 1))
                        ffn_chunk(0, W1B, c, FROWS[c])
                    if n == 6 and live(g - 1, BODIES):
                        wait(pe, x2_ready, g)
                        transposes(g, "ln", n, x2[:, :], tlf)
                    if live(unit(g, n, T_LAG), NUNITS):
                        scores(g, n)
                    if live(unit(g, n, P_LAG), NUNITS):
                        attend(g, n)

            bodies(pe, body)

            def prepare(b, j, piece):
                if piece == 0:
                    pe.wait_ge(l_norm, b + 1)
                    wait(pe, l_acc, b)
                    for t in range(TILES):
                        m = nc.tensor.transpose(ps[:, 0, t * 128:t * 128 + 128], xt[:, t, :], ident[:, :])
                    m.then_inc(l_tr, 1)
                elif piece == 1:
                    pe.wait_ge(l_cp, b + 1)
                    wait(pe, l_ev, b * 3)
                    nc.tensor.matmul(ps[0:DQ, 1, :], wq_sb[:, 0, :], xn[:, :], start=True, stop=True).then_inc(l_mm, 1)
                    nc.tensor.matmul(ps[0:DQ, 0, :], wq_sb[:, 1, :], xn[:, :], start=True, stop=True).then_inc(l_mm, 1)
                elif piece == 2:
                    pe.wait_ge(l_ev, b * 3 + 1)
                    for t in range(TILES):
                        m = nc.tensor.matmul(ps[:, 1, t * 128:t * 128 + 128], xn[:, t * 128:t * 128 + 128], wv_sb[:, :], start=True, stop=True)
                    m.then_inc(l_mm, 1)
                    pe.wait_ge(l_ev, b * 3 + 2)
                    pe.wait_ge(l_fs, b + 1)
                    for t in range(TILES):
                        m = nc.tensor.transpose(ps[:, 0, t * 128:t * 128 + 128], last_f[:, t * 128:t * 128 + 128], ident[:, :])
                    m.then_inc(l_ft, 1)

            def last(b, j, pair):
                for t in range(TILES):
                    T = b * TILES + t
                    if live(b, BATCH):
                        keys = (t + 1) * 128
                        pe.wait_ge(l_ev, b * 3 + 2)
                        wait(pe, l_ex, T - 1)
                        nc.tensor.matmul(ps[:, 4 + t % 2, 0:keys], ident_b[:, :], mask_c[:, SEQ - keys:SEQ], start=True, stop=False, skip_group_check=True)
                        nc.tensor.matmul(ps[:, 4 + t % 2, 0:keys], last_q[:, j, t * 128:t * 128 + 128], last_k[:, j, 0:keys], start=False, stop=True, skip_group_check=True).then_inc(l_s, 1)
                    if live(b + 1, BATCH):
                        prepare(b + 1, 1 - j, t)
                    if live(T - 1, BATCH * TILES):
                        s = (t - 1) % 2
                        pe.wait_ge(l_ex, T)
                        wait(pe, l_pc, T - 2)
                        for c in range((t - 1) % TILES + 1):
                            m = nc.tensor.transpose(ps[:, 2 + s, c * 128:c * 128 + 128], last_p[:, s, c * 128:c * 128 + 128], ident[:, :])
                        m.then_inc(l_pt, 1)
                    if live(T - 2, BATCH * TILES):
                        u, s, jj = (t - 2) % TILES, t % 2, j if t >= 2 else 1 - j
                        pe.wait_ge(l_pc, T - 1)
                        if u == 0:
                            pe.wait_ge(l_ev, b * 3 + 3)
                        wait(pe, l_res, T - 3)
                        for c in range(u + 1):
                            m = nc.tensor.matmul(ps[:, 6 + s, 0:128], last_pT[:, s, c * 128:c * 128 + 128], last_v[:, jj, c, :], start=c == 0, stop=c == u)
                        m.then_inc(l_o, 1)

            pe.wait_ge(l_w, 48)
            for piece in range(3):
                prepare(0, 0, piece)
            last_batches(pe, last)

        @block.scalar
        def _(act):
            act.preload_act_table(ACT.Exp)
            act.wait_ge(zeroed, 1)
            def first(b, j, pair):
                act.wait_ge(f_tr, b + 1)
                nc.scalar.activation(state(b, 0, SEQ, slice(0, 64)), ps[0:64, T_BANK[j], :], ACT.Copy)
                nc.scalar.activation(state(b, 1, SEQ, slice(64, 128)), ps[64:128, T_BANK[j], :], ACT.Copy).then_inc(f_cp, 1)

            pairs(act, first)

            def high_part(g, b, layer, t):
                if isinstance(layer, int):
                    act.wait_ge(f_cp, BATCH)
                else:
                    act.wait_ge(res2, g - (BATCH - 1))
                wait(act, projected, (g * UPB + 2 * t - UPB + 2) * 3)
                nc.scalar.activation(xh[:, t * 128:t * 128 + 128], state(b, t * 128, 128), ACT.Copy).then_inc(xh_ready, 1)

            def high_weights(g, layer, h):
                if not isinstance(layer, int):
                    act.wait_ge(projected, (unit(g, h, 2) + 1) * 3)
                for kind in range(3):
                    dst, src = chunk(wqkv_hi, kind, h), raw_chunk(kind, h)
                    nc.scalar.activation(view_v(dst) if kind == 2 else dst, src, ACT.Copy).then_inc(wsplit_hi, 1)

            def square(g, n, kind):
                u = unit(g, n, 0)
                act.wait_ge(projected, 3 * u + kind + 1)
                wait(act, reduced, 2 * u + kind - 1)
                x = ps[:, P_BANK[(3 * n + kind) % 2], :]
                nc.scalar.activation(sq[:, kind, :], x, ACT.Square).then_inc(squared, 1)
                wait(act, summed, 2 * (u - 2) + kind + 1)
                nc.scalar.activation(t1[:, slot(n, 0, 2), kind, :], x, ACT.Copy).then_inc(qk_copied, 1)

            def body(g, b, layer):
                peeled = isinstance(b, int)
                for n in range(UPB):
                    now, ffn = live(unit(g, n, 0), NUNITS), live(g - 2, BODIES)
                    if peeled and b == 0 and layer is not None and n == 0:
                        act.wait_ge(raw_in, layer * 16 + 16)
                        high_weights(g, layer, 0)
                    if n == 0 and now:
                        high_part(g, b, layer, 0)
                    if now:
                        square(g, n, 0)
                    if live(unit(g, n, P_LAG), NUNITS):
                        u, s = unit(g, n, P_LAG), slot(n, P_LAG, 2)
                        act.wait_ge(subbed, u + 1)
                        wait(act, tp, u - 1)
                        wait(act, sumd, u - 1)
                        nc.scalar.activation(prob[:, s, :].rearrange("p (a b c) -> p b a c", a=4, b=2),
                                             dsub[:, s, :].rearrange("p (b a c) -> p b a c", a=4, b=2), ACT.Exp, scale=8.0).then_inc(expd, 1)
                    if live(unit(g, n, T_LAG), NUNITS):
                        u, s = unit(g, n, T_LAG), slot(n, T_LAG, 2)
                        act.wait_ge(tq, u + 1)
                        wait(act, scored, u - 1)
                        nc.scalar.activation(qT[:, s, :, :].rearrange("p a b -> p (a b)"), ps[:, t_bank("q", n), :], ACT.Copy).then_inc(cq, 1)
                    if live(unit(g, n, T_LAG), NUNITS):
                        u, h, ts = unit(g, n, T_LAG), half(n, T_LAG), tslot(n, T_LAG) % 2
                        src = ps[:, t_bank("k", n), :].rearrange("p (a b) -> p a b", a=4)
                        act.wait_ge(tk, u + 1)
                        wait(act, scored, u - 1)
                        nc.scalar.activation(kT[:, h, ts, :, WIN:], src, ACT.Copy)
                        nc.scalar.activation(kT[:, h, 1 - ts, :, 0:WIN], src[:, :, 128 - WIN:], ACT.Copy).then_inc(ck, 1)
                    if n in (2, 3, 4) and ffn:
                        c = n - 2
                        rows = FROWS[c]
                        act.wait_ge(gate_done, (g - 2) * NFC + (c + 1))
                        if c == 0:
                            if not peeled or b == 2:
                                act.wait_ge(ffp_in, (layer + 1) * 160)
                            wait(act, hid_done, g - 2)
                        nc.scalar.activation(gate[0:rows, c, :], W1B[0:rows, :], ACT.Identity, bias=b1_sb[0:rows, 1, c:c + 1]).then_inc(gate_copied, 1)
                    if live(unit(g, n, P_LAG), NUNITS):
                        u, s = unit(g, n, P_LAG), slot(n, P_LAG, 2)
                        act.wait_ge(tp, u + 1)
                        wait(act, attended, u - 1)
                        nc.scalar.activation(pT[:, s, :, :].rearrange("p a b -> p (a b)"), ps[:, t_bank("p", n), :], ACT.Copy).then_inc(cp, 1)
                    if n == 6 and live(g - 1, BODIES):
                        act.wait_ge(res1, g * TILES)
                        wait(act, tlf, g - 1)
                        nc.scalar.activation(x2[:, :], state(prev_batch(b, 1), 0, SEQ), ACT.Copy).then_inc(x2_ready, 1)
                    if now:
                        u, par, ts = unit(g, n, 0), half(n, 0), tslot(n, 0) % 2
                        act.wait_ge(projected, 3 * u + 3)
                        if par == 0:
                            before = g * 2 + n // 4
                            wait(act, vw_ready[ts], before * 128)
                            wait(act, vw_edge[1 - ts], (before + ts) * 32)
                        nc.scalar.activation(v_sb[:, ts, par, :], ps[:, P_BANK[(3 * n + 2) % 2], :], ACT.Copy).then_inc(v_copied, 1)
                        if n % 2 == 1 and n < UPB - 1:
                            high_part(g, b, layer, (n + 1) // 2)
                    if now:
                        square(g, n, 1)
                    if n == 1 and ffn:
                        if not peeled or b == 2:
                            act.wait_ge(lnp_in, (layer + 1) * 32)
                        act.wait_ge(tlb, g - 1)
                        wait(act, xnl_ready, g - 2)
                        nc.scalar.activation(xn[:, :], ps[:, t_bank("lnb", 1), :], ACT.Identity, bias=lnb_sb[:, 0:1], scale=lng_sb[:, 0:1]).then_inc(clb, 1)
                        wait(act, a_done, (g - 2) * NFC)
                        act.wait_ge(clb, g - 1)
                        nc.scalar.activation(xn_hi[:, :], xn[:, :], ACT.Copy).then_inc(xnh_ready, 1)
                    if peeled and b == 1 and layer is not None and n == 5:
                        act.wait_ge(w1raw_in, layer * 16 + 16)
                        if not isinstance(layer, int):
                            act.wait_ge(a_done, layer * (BATCH * NFC))
                        nc.scalar.activation(w1_hi[:, :], w1_raw[:, :], ACT.Copy).then_inc(w1_hi_ready, 1)
                    if live(unit(g, n, O_LAG), NUNITS):
                        u, h = unit(g, n, O_LAG), half(n, O_LAG)
                        act.wait_ge(to, u + 1)
                        if h == 0:
                            wait(act, wo_done, tile2(g, n) - 1)
                        nc.scalar.activation(oT[:, tslot(n, O_LAG) % 2, 4 * h:4 * h + 4, :].rearrange("p a b -> p (a b)"),
                                             ps[:, t_bank("o", n), :], ACT.Copy).then_inc(co, 1)
                    if n == 4 and ffn:
                        act.wait_ge(gate_copied, (g - 2) * NFC + NFC)
                        nc.scalar.activation(gate[:, :, :].rearrange("p a b -> p (a b)"), gate[:, :, :].rearrange("p a b -> p (a b)"), ACT.Gelu).then_inc(gelu_done, 1)
                    if n in (2, 3, 4) and ffn:
                        c = n - 2
                        rows = FROWS[c]
                        act.wait_ge(a_done, (g - 2) * NFC + (c + 1))
                        if c == 0:
                            wait(act, down_done, g - 2)
                        nc.scalar.activation(hid[0:rows, c, :], W1B[0:rows, :], ACT.Identity, bias=b1_sb[0:rows, 0, c:c + 1]).then_inc(a_copied, 1)
                    if peeled and b == 0 and layer is not None and n == 0:
                        high_weights(g, layer, 1)
                    if n == 6 and live(g - 1, BODIES):
                        act.wait_ge(tlf, g)
                        wait(act, tlb, g - 1)
                        nc.scalar.activation(xt[:, :, :].rearrange("p t d -> p (t d)"), ps[:, t_bank("ln", 6), :], ACT.Copy).then_inc(clf, 1)

            def tile2(g, n):
                return g * TILES + (n - O_LAG) // 2

            bodies(act, body)

            def prepare(b, j, piece):
                if piece == 0:
                    act.wait_ge(l_tr, b + 1)
                    wait(act, l_mm, b * 3)
                    nc.scalar.activation(xn[:, :], ps[:, 0, :], ACT.Copy).then_inc(l_cp, 1)
                elif piece == 1:
                    wait(act, l_ft, b)
                    nc.scalar.activation(last_f[0:64, :], state(b, 0, SEQ, slice(0, 64)), ACT.Copy)
                    nc.scalar.activation(last_f[64:128, :], state(b, 1, SEQ, slice(64, 128)), ACT.Copy).then_inc(l_fs, 1)
                    act.wait_ge(l_mm, b * 3 + 1)
                    wait(act, l_s, (b - 1) * TILES)
                    nc.scalar.activation(last_q[:, j, :], ps[0:DQ, 1, :], ACT.Copy).then_inc(l_ev, 1)
                    act.wait_ge(l_mm, b * 3 + 2)
                    nc.scalar.activation(last_k[:, j, :], ps[0:DQ, 0, :], ACT.Copy).then_inc(l_ev, 1)
                elif piece == 2:
                    act.wait_ge(l_mm, b * 3 + 3)
                    wait(act, l_o, (b - 1) * TILES)
                    nc.scalar.activation(last_v[:, j], ps[:, 1, :].rearrange("p (t d) -> p t d", t=TILES), ACT.Copy).then_inc(l_ev, 1)

            def last(b, j, pair):
                for t in range(TILES):
                    T = b * TILES + t
                    if live(b, BATCH):
                        keys = (t + 1) * 128
                        act.wait_ge(l_ng, T + 1)
                        wait(act, l_pt, T - 1)
                        wait(act, l_iv, T - 3)
                        nc.scalar.activation(last_p[:, t % 2, 0:keys], ps[:, 4 + t % 2, 0:keys], ACT.Exp, bias=smax[:, 1, t:t + 1],
                                             scale=1 / math.sqrt(DQ), accum_out=rsum[:, 0, t:t + 1]).then_inc(l_ex, 1)
                    if live(b + 1, BATCH):
                        prepare(b + 1, 1 - j, t)
                    if live(T - 1, BATCH * TILES):
                        s, keys = (t - 1) % 2, ((t - 1) % TILES + 1) * 128
                        act.wait_ge(l_pt, T)
                        wait(act, l_o, T - 2)
                        nc.scalar.activation(last_pT[:, s, 0:keys], ps[:, 2 + s, 0:keys], ACT.Copy).then_inc(l_pc, 1)

            for piece in range(3):
                prepare(0, 0, piece)
            last_batches(act, last)

        @block.vector
        def _(dve):
            def rsqrt_step(k, x, y, tmp, done, before):
                if k > 0:
                    dve.wait_ge(done, before + k)
                if k == 0:
                    i = nc.vector.tensor_scalar(tmp.bitcast(I32), x.bitcast(I32), 1, None, ALU.logical_shift_right)
                elif k == 1:
                    i = nc.vector.tensor_scalar(y.bitcast(I32), tmp.bitcast(I32), -1.0, SQRT_MAGIC, ALU.mult, ALU.add)
                elif k % 3 == 2:
                    i = nc.vector.tensor_tensor(tmp, y, y, ALU.mult)
                elif k % 3 == 0:
                    i = nc.vector.scalar_tensor_tensor(tmp, tmp, -0.5, x, ALU.mult, ALU.mult)
                else:
                    i = nc.vector.scalar_tensor_tensor(y, tmp, 1.5, y, ALU.add, ALU.mult)
                i.then_inc(done, 1)

            def ln_statistics(src, s_bn, s_ag, s_out, i):
                wait(dve, s_out, i)
                for t in range(TILES):
                    nc.vector.bn_stats(bst[:, t, :], src[:, t, :]).then_inc(s_bn, 1)
                dve.wait_ge(s_bn, i * TILES + TILES)
                nc.vector.memset(lnv[:, :], 1e-5).then_inc(s_ag, 1)
                for t in range(TILES):
                    nc.vector.bn_aggr(mv[:, t, :], bst[:, t, :]).then_inc(s_ag, 1)
                dve.wait_ge(s_ag, i * 6 + 5)
                nc.vector.tensor_tensor(lnv[:, :], lnv[:, :], mv[:, :, 1], ALU.add).then_inc(s_ag, 1)

            def ln_newton_step(k, s_ag, s_nw, i):
                if k == 0:
                    dve.wait_ge(s_ag, i * 6 + 6)
                rsqrt_step(k, lnv[:, :], lnr[:, :], lnt[:, :], s_nw, i * NEWTON)

            def ln_normalise(src, dst, s_nw, s_out, i):
                dve.wait_ge(s_nw, i * NEWTON + NEWTON)
                for t in range(TILES):
                    m = nc.vector.tensor_scalar(dst[:, t, :], src[:, t, :], mv[:, t, 0:1], lnr[:, t:t + 1], ALU.subtract, ALU.mult)
                m.then_inc(s_out, 1)

            def first(b, j, pair):
                dve.wait_ge(x_in[j], pair * 16 + 16)
                ln_statistics(xin[:, j], f_bn, f_ag, f_norm, b)
                for k in range(NEWTON):
                    ln_newton_step(k, f_ag, f_newton, b)
                wait(dve, f_tr, b - 1)
                ln_normalise(xin[:, j], qk[:, j, 0, :].rearrange("p (t d) -> p t d", t=TILES), f_newton, f_norm, b)

            pairs(dve, first)

            def rotary(g, n, kind):
                u, s, t = unit(g, n, 0), slot(n, 0, 2), tslot(n, 0)
                x = ps[:, P_BANK[(3 * n + kind) % 2], :].rearrange("p (h a d) -> p h a d", a=2, d=DH // 2)[:, :, ::-1, :]
                sin = rot[:, 2 * kind + 1, t, :].rearrange("p (o a d) -> p o a d", o=1, a=2).to_broadcast([128, 8, 2, DH // 2])
                dve.wait_ge(qk_copied, 2 * u + kind + 1)
                wait(dve, summed, 2 * (u - 2) + kind + 1)
                nc.vector.tensor_tensor(t2[:, s, kind, :].rearrange("p (h a d) -> p h a d", a=2, d=DH // 2), x, sin, ALU.mult).then_inc(rotated, 1)

            def sums_of_squares(g, n, kind):
                u, s = unit(g, n, 0), slot(n, 0, 2)
                dve.wait_ge(squared, 2 * u + kind + 1)
                if kind == 0:
                    wait(dve, newton, (u - 1) * NEWTON)
                nc.vector.tensor_reduce(n2[:, s, 8 * kind:8 * kind + 8], view_v(sq[:, kind, :]), AX.X, ALU.add).then_inc(reduced, 1)

            def norm_step(g, n, k):
                u = unit(g, n, 1)
                if live(u, NUNITS):
                    if k == 0:
                        dve.wait_ge(reduced, 2 * u + 2)
                        wait(dve, normed, 2 * (u - 3))
                    rsqrt_step(k, n2[:, slot(n, 1, 2), :], rn[:, slot(n, 1, 4), :], nwt[:, :], newton, u * NEWTON)

            def clamp(g, n):
                u = unit(g, n, 1)
                if live(u, NUNITS):
                    dve.wait_ge(reduced, 2 * u + 2)
                    x = n2[:, slot(n, 1, 2), :]
                    nc.vector.tensor_scalar(x, x, 1e-24, None, ALU.max).then_inc(clamped, 1)
                    dve.wait_ge(clamped, u + 1)

            def low_weights(layer, h):
                for kind in range(3):
                    dve.wait_ge(wsplit_hi, layer * 6 + (3 * h + kind + 1))
                    lo, hi, raw = chunk(wqkv_lo, kind, h), chunk(wqkv_hi, kind, h).bitcast(F32), raw_chunk(kind, h)
                    if kind == 2:
                        lo, hi = view_v(lo), view_v(hi)
                    nc.vector.tensor_tensor(lo, raw, hi, ALU.subtract).then_inc(wsplit_lo, 1)

            def body(g, b, layer):
                peeled = isinstance(b, int)
                for n in range(UPB):
                    now = live(unit(g, n, 0), NUNITS)
                    ffn = live(g - 2, BODIES)
                    if peeled and b == 0 and layer is not None and n == 0:
                        low_weights(layer, 0)
                        wait(dve, rotated, g * (2 * UPB))
                        wait(dve, cos_done, g * (2 * UPB))
                        if isinstance(layer, int):
                            dve.wait_ge(const_in, CONSTS * 16)
                        for i in range(4):
                            sc = qks[:, i, bass.ds(layer, 1), :].to_broadcast([128, TILES, DH])
                            m = nc.vector.tensor_tensor(rot[:, i, :, :], rot_base[:, i, :, :], sc, ALU.mult)
                        m.then_inc(rot_ready, 1)
                        dve.wait_ge(rot_ready, layer + 1)
                    if now:
                        rotary(g, n, 0)
                    clamp(g, n)
                    if live(unit(g, n, O_LAG), NUNITS):
                        u, s = unit(g, n, O_LAG), slot(n, O_LAG, 2)
                        dve.wait_ge(attended, u + 1)
                        dve.wait_ge(inverted, u + 1)
                        wait(dve, to, u - 1)
                        O = ps[:, S_BANK:S_BANK + 2, 256:512].rearrange("p b (a c) -> p a b c", a=4)
                        nc.vector.tensor_tensor(o_sb[:, s, :].rearrange("p (a b c) -> p a b c", a=4, b=2), O,
                                                rinv[:, s, :].rearrange("p (a b o) -> p a b o", b=2, o=1).to_broadcast([128, 4, 2, 64]), ALU.mult).then_inc(o_copied, 1)
                    step(g, n, 0)
                    if n == 1 and ffn:
                        ln_normalise(xt, xt, ln_newton, xt_normed, g - 2)
                    if now:
                        sums_of_squares(g, n, 0)
                    step(g, n, 1)
                    if live(unit(g, n, P_LAG), NUNITS):
                        u, s = unit(g, n, P_LAG), slot(n, P_LAG, 2)
                        dve.wait_ge(expd, u + 1)
                        wait(dve, inverted, u - 1)
                        nc.vector.tensor_reduce(rsum[:, s, :], view_v(prob[:, s, :]), AX.X, ALU.add).then_inc(sumd, 1)
                    step(g, n, 2)
                    step(g, n, 3)
                    step(g, n, 4)
                    if n % 2 == 1 and live(tile1(g, n), NTILES):
                        T, t = tile1(g, n), (n - WO_LAG) // 2 % TILES
                        bb = b if n == 7 else prev_batch(b, 1)
                        dve.wait_ge(wo_done, T + 1)
                        lo, hi = state(bb, t * 128, 128, slice(0, 64)), state(bb, t * 128 + 1, 128, slice(64, 128))
                        nc.vector.tensor_tensor(lo, lo, W0[0:64, 0:128], ALU.add)
                        nc.vector.tensor_tensor(hi, hi, W0[64:128, 0:128], ALU.add).then_inc(res1, 1)
                    step(g, n, 5)
                    if n == 5 and ffn:
                        dve.wait_ge(gelu_done, g - 1)
                        dve.wait_ge(a_copied, (g - 2) * NFC + NFC)
                        for c, rows in enumerate(FROWS):
                            m = nc.vector.tensor_tensor(hid[0:rows, c, :], hid[0:rows, c, :], gate[0:rows, c, :], ALU.mult)
                        m.then_inc(hid_done, 1)
                    if now:
                        rotary(g, n, 1)
                    step(g, n, 6)
                    if now:
                        sums_of_squares(g, n, 1)
                    step(g, n, 7)
                    if peeled and b == 1 and layer is not None and n == 5:
                        dve.wait_ge(w1_hi_ready, layer + 1)
                        nc.vector.tensor_tensor(w1_lo[:, :], w1_raw[:, :], w1_hi[:, :].bitcast(F32), ALU.subtract).then_inc(w1_lo_ready, 1)
                    if n == 6 and ffn:
                        bb = prev_batch(b, 2)
                        dve.wait_ge(down_done, g - 1)
                        lo, hi = state(bb, 0, SEQ, slice(0, 64)), state(bb, 1, SEQ, slice(64, 128))
                        nc.vector.scalar_tensor_tensor(lo, W1B[0:64, :], b2_sb[0:64, 0:1], lo, ALU.add, ALU.add)
                        nc.vector.scalar_tensor_tensor(hi, W1B[64:128, :], b2_sb[64:128, 0:1], hi, ALU.add, ALU.add).then_inc(res2, 1)
                    if n == 7 and live(g - 1, BODIES):
                        dve.wait_ge(clf, g)
                        ln_statistics(xt, bn_done, ag_done, xt_normed, g - 1)
                    if peeled and b == 0 and layer is not None and n == 0:
                        low_weights(layer, 1)
                    step(g, n, 8)
                    if live(unit(g, n, P_LAG), NUNITS):
                        u, s = unit(g, n, P_LAG), slot(n, P_LAG, 2)
                        dve.wait_ge(sumd, u + 1)
                        wait(dve, o_copied, u - 1)
                        nc.vector.reciprocal(rinv[:, s, :], rsum[:, s, :]).then_inc(inverted, 1)
                    step(g, n, 9)
                    step(g, n, 10)
                    if n == 1 and ffn:
                        dve.wait_ge(xnh_ready, g - 1)
                        nc.vector.tensor_tensor(xn_lo[:, :], xn[:, :], xn_hi[:, :].bitcast(F32), ALU.subtract).then_inc(xnl_ready, 1)
                    if live(unit(g, n, T_LAG), NUNITS):
                        u, s = unit(g, n, T_LAG), slot(n, T_LAG, 2)
                        dve.wait_ge(scored, u + 1)
                        if live(unit(g, n, P_LAG), NUNITS):
                            dve.wait_ge(attended, u)
                        S = ps[:, S_BANK:S_BANK + 2, 0:256].rearrange("p b (a c) -> p b a c", a=4)
                        nc.vector.tensor_reduce(smax[:, s, :].rearrange("p (b a) -> p b a", b=2), S, AX.X, ALU.max).then_inc(maxed, 1)
                        dve.wait_ge(maxed, u + 1)
                        wait(dve, expd, u - 1)
                        nc.vector.tensor_tensor(dsub[:, s, :].rearrange("p (b a c) -> p b a c", a=4, b=2), S,
                                                smax[:, s, :].rearrange("p (b a o) -> p b a o", b=2, o=1).to_broadcast([128, 2, 4, 64]), ALU.subtract).then_inc(subbed, 1)

            def step(g, n, k):
                norm_step(g, n, k)
                if n == 0 and live(g - 2, BODIES):
                    ln_newton_step(k, ag_done, ln_newton, g - 2)

            def tile1(g, n):
                return g * TILES + (n - WO_LAG) // 2

            bodies(dve, body)

            def normalise(b, j, count, piece):
                if piece == 1:
                    dve.wait_ge(l_x[j], count * 16 + 16)
                    ln_statistics(xin[:, j], l_bn, l_ag, l_norm, b)
                if piece < 3:
                    for k in range(NEWTON)[5 * piece - 5:5 * piece if piece == 1 else NEWTON]:
                        ln_newton_step(k, l_ag, l_newton, b)
                else:
                    wait(dve, l_tr, b)
                    ln_normalise(xin[:, j], xt, l_newton, l_norm, b)

            def accumulate(b, j):
                dve.wait_ge(l_ft, b + 1)
                wait(dve, l_res, (b - 1) * TILES)
                nc.vector.tensor_tensor(last_acc[:, j, :], ps[:, 0, :], xin[:, j].rearrange("p t d -> p (t d)"), ALU.add).then_inc(l_acc, 1)

            def last(b, j, pair):
                for t in range(TILES):
                    T = b * TILES + t
                    if live(b, BATCH):
                        keys = (t + 1) * 128
                        dve.wait_ge(l_s, T + 1)
                        wait(dve, l_ex, T - 3)
                        nc.vector.tensor_reduce(smax[:, 0, t:t + 1], ps[:, 4 + t % 2, 0:keys], AX.X, ALU.max).then_inc(l_mx, 1)
                        dve.wait_ge(l_mx, T + 1)
                        nc.vector.tensor_scalar(smax[:, 1, t:t + 1], smax[:, 0, t:t + 1], -1 / math.sqrt(DQ), None, ALU.mult).then_inc(l_ng, 1)
                    if live(T - 1, BATCH * TILES):
                        u = (t - 1) % TILES
                        dve.wait_ge(l_ex, T)
                        wait(dve, l_res, T - 4)
                        nc.vector.reciprocal(rinv[:, 0, u:u + 1], rsum[:, 0, u:u + 1]).then_inc(l_iv, 1)
                    if t > 0 and live(b + 2, BATCH):
                        normalise(b + 2, j, pair + 1, t)
                    if t == 3 and live(b + 1, BATCH):
                        accumulate(b + 1, 1 - j)
                    if live(T - 2, BATCH * TILES):
                        u, jj = (t - 2) % TILES, j if t >= 2 else 1 - j
                        dve.wait_ge(l_o, T - 1)
                        dve.wait_ge(l_iv, T - 1)
                        if u == 0:
                            dve.wait_ge(l_acc, b + 1)
                            wait(dve, l_out[j], pair * 16)
                        nc.vector.scalar_tensor_tensor(last_o[:, jj, u * 128:u * 128 + 128], ps[:, 6 + t % 2, 0:128], rinv[:, 0, u:u + 1],
                                                       last_acc[:, jj, u * 128:u * 128 + 128], ALU.mult, ALU.add).then_inc(l_res, 1)

            for b in range(2):
                for piece in range(1, 4):
                    normalise(b, b, 0, piece)
            accumulate(0, 0)
            last_batches(dve, last)

        @block.gpsimd
        def _(pool):
            for buf in (xs, kT, v_sb, gate):
                last = nc.gpsimd.memset(buf[:], 0.0)
            last.then_inc(zeroed, 1)

            def low_part(g, b, t):
                pool.wait_ge(xh_ready, g * TILES + (t + 1))
                nc.gpsimd.tensor_tensor(xl[:, t * 128:t * 128 + 128], state(b, t * 128, 128), xh[:, t * 128:t * 128 + 128].bitcast(F32), ALU.subtract).then_inc(xl_ready, 1)

            def add(g, n, kind):
                u, s = unit(g, n, 0), slot(n, 0, 2)
                t, x = tslot(n, 0), view_v(t1[:, s, kind, :])
                pool.wait_ge(qk_copied, 2 * u + kind + 1)
                cos = rot[:, 2 * kind, t, :].rearrange("p (o d) -> p o d", o=1).to_broadcast([128, 8, DH])
                nc.gpsimd.tensor_tensor(x, x, cos, ALU.mult).then_inc(cos_done, 1)
                pool.wait_ge(cos_done, 2 * u + kind + 1)
                pool.wait_ge(rotated, 2 * u + kind + 1)
                wait(pool, tk if kind else tq, u - 3)
                nc.gpsimd.tensor_tensor(qk[:, slot(n, 0, 4), kind, :], t1[:, s, kind, :], t2[:, s, kind, :], ALU.add).then_inc(summed, 1)

            def mul(g, n, kind):
                u, s = unit(g, n, 2), slot(n, 2, 4)
                pool.wait_ge(newton, (u + 1) * NEWTON)
                pool.wait_ge(summed, 2 * u + kind + 1)
                x = view_v(qk[:, s, kind, :])
                r = rn[:, s, 8 * kind:8 * kind + 8].rearrange("p (h o) -> p h o", o=1).to_broadcast([128, 8, DH])
                nc.gpsimd.tensor_tensor(x, x, r, ALU.mult).then_inc(normed, 1)

            def body(g, b, layer):
                for n in range(UPB):
                    if n == 0 and live(unit(g, n, 0), NUNITS):
                        low_part(g, b, 0)
                    if live(unit(g, n, 2), NUNITS):
                        mul(g, n, 0)
                        mul(g, n, 1)
                    if isinstance(b, int) and b == 0 and n == 0 and layer is not None:
                        pool.wait_ge(rot_ready, layer + 1)
                    if live(unit(g, n, 0), NUNITS):
                        add(g, n, 0)
                        if n % 2 == 1 and n < UPB - 1:
                            low_part(g, b, (n + 1) // 2)
                        add(g, n, 1)

            bodies(pool, body)


_INS = ["L0_attn_X", "L0_attn_Wq", "L0_attn_Wk", "L0_attn_Wv", "L0_ffn_Wqkv", "L0_ffn_q_scale", "L0_ffn_k_scale",
        "L0_ffn_Wo", "L0_ffn_ln_g", "L0_ffn_ln_b", "L0_ffn_W1", "L0_ffn_b1", "L0_ffn_W2", "L0_ffn_b2"]


def constants():
    f = np.float32
    halfd = np.arange(0, DH, 2, dtype=f)
    inv_freq = (f(1.0) / f(10000.0) ** (halfd / f(DH))).astype(f)
    tok = np.arange(SEQ, dtype=f)
    freqs = np.concatenate([tok[:, None] * inv_freq[None, :]] * 2, -1).astype(f)
    base = ((halfd + f(0.4 * DH)) / f(1.4 * DH)).astype(f)
    power = ((tok - f(SEQ // 2)) / f(WIN // 2)).astype(f)
    scale = np.concatenate([(base[None, :] ** power[:, None]).astype(f)] * 2, -1)
    cos, sin = np.cos(freqs), np.sin(freqs)
    sign = np.where(np.arange(DH) < DH // 2, f(-1), f(1))
    tables = np.stack([cos * scale, sin * scale * sign, cos / scale, sin / scale * sign]).astype(f)
    tables = tables.reshape(4, TILES, 128, DH).transpose(2, 0, 1, 3)
    q, c = np.arange(128)[:, None], np.arange(2 * WIN)[None, :]
    ok = (c >= q % WIN) & (c <= q % WIN + WIN)
    first = ok & ((q >= WIN) | (c >= WIN))
    window = np.where(np.stack([first, ok], 1), 0.0, MASKED)
    window = np.tile(window[:, :, None, :], (1, 1, 4, 1)).reshape(128, 2, 256)
    causal = np.zeros((128, SEQ))
    causal[:, SEQ - 128:] = np.where(np.arange(128)[None, :] <= q, 0.0, MASKED)
    bf = mybir.dt.np(BF16)
    return {"rot_tables": np.ascontiguousarray(tables), "window_mask": window.astype(bf), "causal_mask": causal.astype(bf),
            "eye": np.eye(128, dtype=f), "eye_bf": np.eye(128).astype(bf)}


def kernel(**inputs):
    import concourse.bacc as bacc
    from concourse.bass_utils import run_bass_kernel_spmd

    nc = bacc.Bacc("TRN2", target_bir_lowering=False, num_devices=1)
    arrays = {n: np.ascontiguousarray(inputs[n]) for n in _INS}
    arrays.update(constants())
    args = [nc.dram_tensor(n, a.shape, mybir.dt.from_np(a.dtype), kind="ExternalInput").ap() for n, a in arrays.items()]
    out = nc.dram_tensor("out", (BATCH, SEQ, DIM), F32, kind="ExternalOutput").ap()
    build(nc, *args, out)
    r = run_bass_kernel_spmd(nc, [arrays], core_ids=[0])
    return r.results[0]["out"]
```
